# Optimizing a Trainium2 kernel written in Bass

```python
import numpy as np
import jax
import jax.numpy as jnp

def _softmax(x, axis=-1):
    return jax.nn.softmax(x, axis=axis)

def _gelu(x):
    return jax.nn.gelu(x, approximate=True)

def _silu(x):
    return jax.nn.silu(x)

def _sigmoid(x):
    return jax.nn.sigmoid(x)

def _layernorm(x, axis=-1, eps=1e-05):
    m = jnp.mean(x, axis=axis, keepdims=True)
    v = jnp.var(x, axis=axis, keepdims=True)
    return (x - m) / jnp.sqrt(v + eps)

def _scatter_add(tgt, idx, src, axis=0):
    return tgt.at[idx].add(src)

def _segment_sum(src, seg, n):
    return jax.ops.segment_sum(src, seg, n)
kernel_name = 'mk_sandwich_d1_jaxref_r2_9a5a61'

def setup_inputs(seed: int=0):
    np.random.seed(seed)
    _w = jnp.asarray

    def _L0_attn_setup():
        import jax, jax.numpy as jnp
        import numpy as np
        HEADS = 16
        key = jax.random.key(seed)
        k1, k2, k3 = jax.random.split(key, 3)
        B, N, C = (4, 2048, 512)
        x = jax.random.normal(k1, (B, N, C), dtype=jnp.float32)
        w_qkv = jax.random.normal(k2, (3 * C, C), dtype=jnp.float32) * C ** (-0.5)
        w_proj = jax.random.normal(k3, (C, C), dtype=jnp.float32) * C ** (-0.5)
        b_proj = jnp.zeros((C,), dtype=jnp.float32)
        return {'x': x, 'w_qkv': w_qkv, 'w_proj': w_proj, 'b_proj': b_proj}
    _L0_attn_in = _L0_attn_setup()

    def _L0_ffn_setup():
        import jax, jax.numpy as jnp
        import numpy as np
        from jax import lax
        H, DK, DV, N_EXP, CHUNK = (8, 64, 64, 4, 64)
        LORA, GATE_LR = (64, 16)
        NORMALIZER = 16.0
        EPS = 1e-05

        def chunk_gla(q, k, v, gk, C=CHUNK):
            L, h, dk = q.shape
            dv = v.shape[-1]
            nc = L // C
            qc, kc, vc, gc = (t.reshape(nc, C, h, -1) for t in (q, k, v, gk))
            g = jnp.cumsum(gc, axis=1)
            g_last = g[:, -1]
            qg = qc * jnp.exp(g)
            kg = kc * jnp.exp(-g)
            A = jnp.einsum('cthd,cshd->chts', qg, kg)
            A = A * jnp.tril(jnp.ones((C, C), q.dtype))
            o_intra = jnp.einsum('chts,cshe->cthe', A, vc)
            k_out = kc * jnp.exp(g_last[:, None] - g)
            chunk_kv = jnp.einsum('cthd,cthe->chde', k_out, vc)
            decay = jnp.exp(g_last)

            def step(S, inp):
                kv, dec, qg_c = inp
                o_inter = jnp.einsum('thd,hde->the', qg_c, S)
                return (S * dec[..., None] + kv, o_inter)
            S0 = jnp.zeros((h, dk, dv), q.dtype)
            _, o_inter = lax.scan(step, S0, (chunk_kv, decay, qg))
            return (o_intra + o_inter).reshape(L, h, dv)
        key = jax.random.key(seed)
        ks = jax.random.split(key, 20)
        B, L, Dh = (1, 2048, 512)
        KD, VD = (H * DK, H * DV)
        w = lambda i, shape: jax.random.normal(ks[i], shape, jnp.float32) * 0.02
        return {'x': jax.random.normal(ks[0], (B, L, Dh), jnp.float32), 'Wq': w(1, (Dh, KD)), 'Wk': w(2, (Dh, KD)), 'Wv': w(3, (Dh, VD)), 'Wqa': w(4, (Dh, LORA)), 'Wqb': w(5, (LORA, KD)), 'Wka': w(6, (Dh, LORA)), 'Wkb': w(7, (LORA, KD)), 'Wg1a': w(8, (Dh, GATE_LR)), 'Wg1b': w(9, (GATE_LR, KD)), 'bg1': jnp.zeros((KD,), jnp.float32), 'Wg2a': w(10, (Dh, GATE_LR)), 'Wg2b': w(11, (GATE_LR, KD)), 'bg2': jnp.zeros((KD,), jnp.float32), 'We': w(12, (Dh, N_EXP)), 'Wga': w(13, (Dh, LORA)), 'Wgb': w(14, (LORA, VD)), 'norm_w': jnp.ones((DV,), jnp.float32), 'Wo': w(15, (VD, Dh))}
    _L0_ffn_in = _L0_ffn_setup()
    _d = {'L0_attn_x': _L0_attn_in['x'], 'L0_attn_w_qkv': _L0_attn_in['w_qkv'], 'L0_attn_w_proj': _L0_attn_in['w_proj'], 'L0_attn_b_proj': _L0_attn_in['b_proj'], 'L0_ffn_Wq': _L0_ffn_in['Wq'], 'L0_ffn_Wk': _L0_ffn_in['Wk'], 'L0_ffn_Wv': _L0_ffn_in['Wv'], 'L0_ffn_Wqa': _L0_ffn_in['Wqa'], 'L0_ffn_Wqb': _L0_ffn_in['Wqb'], 'L0_ffn_Wka': _L0_ffn_in['Wka'], 'L0_ffn_Wkb': _L0_ffn_in['Wkb'], 'L0_ffn_Wg1a': _L0_ffn_in['Wg1a'], 'L0_ffn_Wg1b': _L0_ffn_in['Wg1b'], 'L0_ffn_bg1': _L0_ffn_in['bg1'], 'L0_ffn_Wg2a': _L0_ffn_in['Wg2a'], 'L0_ffn_Wg2b': _L0_ffn_in['Wg2b'], 'L0_ffn_bg2': _L0_ffn_in['bg2'], 'L0_ffn_We': _L0_ffn_in['We'], 'L0_ffn_Wga': _L0_ffn_in['Wga'], 'L0_ffn_Wgb': _L0_ffn_in['Wgb'], 'L0_ffn_norm_w': _L0_ffn_in['norm_w'], 'L0_ffn_Wo': _L0_ffn_in['Wo']}
    _x0 = _d['L0_attn_x']
    _d['L0_attn_x'] = jax.random.normal(jax.random.fold_in(jax.random.key(seed), 1), (2, 4096, 512), dtype=_x0.dtype)
    del _x0
    return _d

def reference(L0_attn_x, L0_attn_w_qkv, L0_attn_w_proj, L0_attn_b_proj, L0_ffn_Wq, L0_ffn_Wk, L0_ffn_Wv, L0_ffn_Wqa, L0_ffn_Wqb, L0_ffn_Wka, L0_ffn_Wkb, L0_ffn_Wg1a, L0_ffn_Wg1b, L0_ffn_bg1, L0_ffn_Wg2a, L0_ffn_Wg2b, L0_ffn_bg2, L0_ffn_We, L0_ffn_Wga, L0_ffn_Wgb, L0_ffn_norm_w, L0_ffn_Wo):

    def _L0_attn_ref(x, w_qkv, w_proj, b_proj):
        import jax, jax.numpy as jnp
        import numpy as np
        HEADS = 16
        B, N, C = x.shape
        H = HEADS
        D = C // H
        qkv = x @ w_qkv.T
        q, k, v = jnp.split(qkv, 3, axis=-1)

        def to_bhdn(t):
            return t.reshape(B, N, H, D).transpose(0, 2, 3, 1)
        q = jax.nn.relu(to_bhdn(q))
        k = jax.nn.relu(to_bhdn(k))
        v = to_bhdn(v)
        eps = jnp.finfo(q.dtype).eps
        ksum = k.sum(axis=-1)
        z = 1.0 / (jnp.einsum('bhd,bhdn->bhn', ksum, q) + eps)
        context = jnp.einsum('bhdn,bhen->bhde', v, k)
        out = jnp.einsum('bhde,bhen->bhdn', context, q)
        out = out * z[:, :, None, :]
        out = out.transpose(0, 3, 1, 2).reshape(B, N, C)
        return out @ w_proj.T + b_proj

    def _L0_ffn_ref(x, Wq, Wk, Wv, Wqa, Wqb, Wka, Wkb, Wg1a, Wg1b, bg1, Wg2a, Wg2b, bg2, We, Wga, Wgb, norm_w, Wo):
        import jax, jax.numpy as jnp
        import numpy as np
        from jax import lax
        H, DK, DV, N_EXP, CHUNK = (8, 64, 64, 4, 64)
        LORA, GATE_LR = (64, 16)
        NORMALIZER = 16.0
        EPS = 1e-05

        def chunk_gla(q, k, v, gk, C=CHUNK):
            L, h, dk = q.shape
            dv = v.shape[-1]
            nc = L // C
            qc, kc, vc, gc = (t.reshape(nc, C, h, -1) for t in (q, k, v, gk))
            g = jnp.cumsum(gc, axis=1)
            g_last = g[:, -1]
            qg = qc * jnp.exp(g)
            kg = kc * jnp.exp(-g)
            A = jnp.einsum('cthd,cshd->chts', qg, kg)
            A = A * jnp.tril(jnp.ones((C, C), q.dtype))
            o_intra = jnp.einsum('chts,cshe->cthe', A, vc)
            k_out = kc * jnp.exp(g_last[:, None] - g)
            chunk_kv = jnp.einsum('cthd,cthe->chde', k_out, vc)
            decay = jnp.exp(g_last)

            def step(S, inp):
                kv, dec, qg_c = inp
                o_inter = jnp.einsum('thd,hde->the', qg_c, S)
                return (S * dec[..., None] + kv, o_inter)
            S0 = jnp.zeros((h, dk, dv), q.dtype)
            _, o_inter = lax.scan(step, S0, (chunk_kv, decay, qg))
            return (o_intra + o_inter).reshape(L, h, dv)
        B, L, Dh = x.shape
        scale = DK ** (-0.5)
        q1 = (x @ Wq).reshape(B, L, H, DK) * scale
        k1 = (x @ Wk).reshape(B, L, H, DK)
        v = (x @ Wv).reshape(B, L, H, DV)
        q2 = (x @ Wqa @ Wqb).reshape(B, L, H, DK) * scale
        k2 = jax.nn.softmax((x @ Wka @ Wkb).reshape(B, L, H, DK), axis=-1)
        gk1 = (jax.nn.log_sigmoid(x @ Wg1a @ Wg1b + bg1) / NORMALIZER).reshape(B, L, H, DK)
        gk2 = (jax.nn.log_sigmoid(x @ Wg2a @ Wg2b + bg2) / NORMALIZER).reshape(B, L, H, DK)
        e = jax.nn.softmax(x @ We, axis=-1)
        _, idx = lax.top_k(e, 1)
        mask = jax.nn.one_hot(idx, N_EXP, dtype=x.dtype).sum(-2)
        rw = e * mask
        fac = jnp.swapaxes(rw, 1, 2)[:, :, :, None, None]
        mfac = jnp.swapaxes(mask, 1, 2)[:, :, :, None, None]
        q_e = q2[:, None] * fac
        k_e = k2[:, None] * fac
        gk_e = gk2[:, None] * mfac
        gla_b = jax.vmap(chunk_gla)
        o_dense = gla_b(q1, k1, v, gk1)
        gla_be = jax.vmap(jax.vmap(chunk_gla, in_axes=(0, 0, None, 0)))
        o_sparse = gla_be(q_e, k_e, v, gk_e).sum(axis=1)
        o = o_dense + o_sparse
        g = (x @ Wga @ Wgb).reshape(B, L, H, DV)
        o = o * lax.rsqrt(jnp.mean(o * o, axis=-1, keepdims=True) + EPS) * norm_w
        o = o * (g * jax.nn.sigmoid(g))
        return o.reshape(B, L, H * DV) @ Wo
    x = L0_attn_x
    x = x + _layernorm(_L0_attn_ref(_layernorm(x, axis=-1), L0_attn_w_qkv, L0_attn_w_proj, L0_attn_b_proj), axis=-1)
    x = x + _layernorm(_L0_ffn_ref(_layernorm(x, axis=-1), L0_ffn_Wq, L0_ffn_Wk, L0_ffn_Wv, L0_ffn_Wqa, L0_ffn_Wqb, L0_ffn_Wka, L0_ffn_Wkb, L0_ffn_Wg1a, L0_ffn_Wg1b, L0_ffn_bg1, L0_ffn_Wg2a, L0_ffn_Wg2b, L0_ffn_bg2, L0_ffn_We, L0_ffn_Wga, L0_ffn_Wgb, L0_ffn_norm_w, L0_ffn_Wo), axis=-1)
    return x

_drawn_inputs = setup_inputs


def setup_inputs(seed=0):
    import zlib

    import numpy as np

    out = dict(_drawn_inputs(seed))
    spreads = {'L0_attn_b_proj': (0.0, 0.1),
     'L0_ffn_bg1': (0.0, 0.1),
     'L0_ffn_bg2': (0.0, 0.8),
     'L0_ffn_norm_w': (1.0, 0.2)}
    factors = {'L0_ffn_Wqa': 8.0,
     'L0_ffn_Wqb': 8.0,
     'L0_ffn_Wka': 8.0,
     'L0_ffn_Wkb': 8.0,
     'L0_ffn_Wg2a': 8.0,
     'L0_ffn_Wg2b': 8.0,
     'L0_ffn_We': 8.0,
     'L0_ffn_Wg1a': 3.699,
     'L0_ffn_Wg1b': 3.988}
    for name, (base, spread) in spreads.items():
        noise = np.random.default_rng([zlib.crc32(name.encode()), seed]).standard_normal(out[name].shape)
        drawn = base * np.exp(spread * noise) if base else spread * noise
        out[name] = jnp.asarray(drawn.astype(out[name].dtype))
    for name, factor in factors.items():
        out[name] = (out[name] * factor).astype(out[name].dtype)
    return out
```

```python
import concourse.bass as bass
from concourse import mybir
from contextlib import ExitStack

BATCH, SEQ, C = 2, 4096, 512
P = 128
KT = C // P
TILES = SEQ // P
GT = 4
GROUPS = TILES // GT
H1, D1 = 16, 32
H2, D2 = 8, 64
PAIRS = H2 // 2
NEXP = 4
REGION = 12804
PATHS = 1 + NEXP
LORA, GLR = 64, 16
ROW_G1, ROW_G2 = LORA, LORA + 32
HALF = P // 2
NORMALIZER = 16.0
EPS = 1e-5
EPS_Z = 1.1920928955078125e-07
W_SCALE = 64.0
S_SCALE = 8.0
REGION2 = 13056
ACT_SET_LN_EXP = 6

CONSTS = {}
_at = 0
for _name, _n in (("ident", P), ("causal", P), ("centred", P), ("halves", 2), ("blocks", P), ("sel_den", KT * P),
                  ("sel_bc", KT * P), ("score", NEXP), ("one_rows", 1), ("ones", P)):
    CONSTS[_name] = (_at, _at + _n)
    _at += _n
N_CONSTS = _at
L_COLS = 2 * P + NEXP


def sandwich_kernel(nc, x_d, wqkv_d, wproj_d, bproj_d, wb_d, wl_d, ws_d, wo_d, nw_d, consts_d, out_d):
    f32, f16 = mybir.dt.float32, mybir.dt.float16
    ALU = mybir.AluOpType
    ACT = mybir.ActivationFunctionType
    X = mybir.AxisListType.X
    q_d = nc.dram_tensor("q_cols", [BATCH * TILES, P, KT * P], f32, kind="Internal").ap()
    x_g = x_d.rearrange("(g t p) c -> g p t c", p=P, t=GT)
    x_p = x_d.rearrange("(j a p) c -> j a p c", p=P, a=2)
    out_p = out_d.rearrange("(j a p) c -> j a p c", p=P, a=2)
    q_p = q_d.rearrange("(j a) p c -> j a p c", a=2)
    q_g = q_d.rearrange("(g t) p c -> g t p c", t=GT)

    with ExitStack() as ctx:
        def sb(name, *shape, dt=f32):
            return ctx.enter_context(nc.sbuf_tensor(name, [P, *shape], dt))

        wqkv = sb("wqkv", 2, KT, 3 * C, dt=f16)
        bproj = sb("bproj", C)
        wb = sb("wb", 2, KT, 3 * C, dt=f16)
        wl = sb("wl", 2, KT, L_COLS, dt=f16)
        ws = sb("ws", 2, 5, C, dt=f16)
        wo = sb("wo", 2, KT, C, dt=f16)
        nw = sb("nw", 1)
        cst = sb("cst", N_CONSTS)
        zero_eps = sb("zero_eps", 1)
        eps_scaled = sb("eps_scaled", 1)
        ident16 = sb("ident16", P, dt=f16)

        def const(name):
            a, b = CONSTS[name]
            return cst[:, a:b]

        ident, causal, centred, halves = const("ident"), const("causal"), const("centred"), const("halves")
        blocks, score, one_rows, ones = const("blocks"), const("score"), const("one_rows"), const("ones")
        sel_den = const("sel_den").rearrange("p (g m) -> p g m", g=KT)
        sel_bc = const("sel_bc").rearrange("p (g m) -> p g m", g=KT)
        CTXW = P + 1
        mix = sb("mix", KT, C)
        kden = sb("kden", KT, P)

        region = sb("region", REGION)
        region2 = sb("region2", REGION2)
        cursor = [0, 0]

        def cut(*shape, own=0, dt=f32):
            n = 1
            for k in shape:
                n *= k
            words = n // 2 if dt == f16 else n
            a = (region, region2)[own][:, cursor[own]:cursor[own] + words]
            cursor[own] += words
            if dt == f16:
                a = a.bitcast(f16)
            if len(shape) == 1:
                return a
            names = "abcd"[:len(shape)]
            return a.rearrange(f"p ({' '.join(names)}) -> p {' '.join(names)}", **dict(zip(names, shape)))

        xn4 = cut(2, GT, C, dt=f16)
        xT4 = cut(2, KT, GT * P, dt=f16)
        q4 = cut(GT, KT, P)
        kk, vv = cut(C), cut(KT, CTXW)
        xf4 = cut(GT, C)
        ctx_sum, ctx_blk = cut(KT, CTXW), cut(KT, P)
        assert cursor[0] <= REGION, cursor
        cursor[0] = GT * C
        w_in = cut(KT, 3 * C)
        cursor[0] = 0
        y, xn = cut(C), cut(2, C, dt=f16)
        xnf = y
        xnT, qz = cut(2, KT, P, dt=f16), cut(KT, P)
        logit_s, lowf, low = cut(4), cut(2, P), cut(2, 2, P, dt=f16)
        gch = cut(3 * C)
        logsig = cut(3, C)
        v, vm = cut(C), cut(NEXP, C)
        ep1, em1, ep2, em2 = cut(C), cut(C), cut(C), cut(C)
        q1g, k1g, q2g, k2g = ep1, em1, ep2, em2
        kd = cut(C)
        q1T, k1T, q2T, k2T = cut(PAIRS, P), cut(PAIRS, P), cut(PAIRS, P), cut(PAIRS, P)
        assert cursor[0] <= REGION, cursor
        qm = cut(NEXP, PAIRS, P, own=1)
        am1, am2 = cut(2, PAIRS, P, own=1), cut(2, PAIRS, P, own=1)
        state = cut(PAIRS, PATHS, P, own=1)
        carry = cut(PAIRS, PATHS, D2, own=1)
        sil, x1 = cut(2, C, own=1), cut(2, C, own=1)
        loaded_at = cursor[1]
        xb, qb, ob = cut(2, C, own=1), cut(2, KT, P, own=1), cut(2, C, own=1)
        assert cursor[1] <= REGION2, cursor
        cursor[1] = loaded_at
        x4 = cut(GT, C, own=1)
        cursor[1] = 0
        wb_in, wl_in, ws_in = cut(KT * 3 * C, own=1), cut(KT * L_COLS, own=1), cut(5 * C, own=1)
        assert cursor[1] <= loaded_at, cursor
        wo_in = mix.rearrange("p a b -> p (a b)")
        cursor[1] = 0
        wproj = cut(KT, C, own=1)
        decay = sb("decay", PAIRS, PATHS)
        exs = sb("exs", 2, PAIRS, PATHS, 2)
        og, og16, ogT = sb("og", C), sb("og16", 2, C, dt=f16), sb("ogT", 2, KT, P, dt=f16)
        osq = og
        same_c, same_d = sb("same_c", P), sb("same_d", P)
        mb = sb("mb", NEXP, P)
        lab_i = sb("lab_i", P)
        z = sb("z", P)
        st = sb("st", 3, 6)
        mv = sb("mv", 3, 2)
        lnv = sb("lnv", 3, 1)
        rstd = sb("rstd", 3, 1)
        lnv1, rstd1 = sb("lnv1", GT, 1), sb("rstd1", GT, 1)
        st1, mv1 = sb("st1", GT, 6), sb("mv1", GT, 2)
        lmax, ldiff, lexp, lsum, rr, rq = sb("lmax", 1), sb("ldiff", 4), sb("lexp", 4), sb("lsum", 1), sb("rr", 1), sb("rq", 1)
        lscore, lab, m4, hm = sb("lscore", 4), sb("lab", 1), sb("m4", 4), sb("hm", NEXP, 2)
        kmax, ksum, krec, kfac = sb("kmax", H2), sb("ksum", H2), sb("krec", H2), sb("kfac", H2)
        oms, oln, ors = sb("oms", H2), sb("oln", H2), sb("ors", H2)

        psum = ctx.enter_context(nc.psum_tensor("psum", [P, 8, 512], f32))
        bank = [psum[:, i, :] for i in range(8)]
        bank16 = [x.bitcast(f16) for x in bank]

        sems = {}

        def S(name):
            if name not in sems:
                sems[name] = ctx.enter_context(nc.semaphore(name))
            return sems[name]

        CREDITS = {
            "scalar": ["xT4_full", "kv0_full", "kv1_full", "q_read",
                       "rstd1_ok", "xnT_ok", "low1_ok", "low0_ok", "lexp_ok", "abs_ok", "ex_ok", "ln_ok", "sig_ok",
                       "v_ok", "ke_ok", "e1_ok", "e2_ok", "exs_ok", "q1T_ok", "k1T_ok", "q2T_ok", "k2T_ok",
                       "osq_ok", "ogT_ok"],
            "vector": ["xn4_ok", "xf4_ok", "low_ok", "ctx_ok", "y_ok", "x1_ok", "xn_ok", "am1_ok", "am2_ok", "carry_ok", "labi_ok",
                       "same_ok", "mb_ok", "ls_ok", "sil_ok", "kd_ok", "kr_ok", "k1g_ok", "q1g_ok", "q2g_ok", "k2g_ok",
                       "z_ok", "qz_ok", "on_ok", "og_ok", "out_ok", "hm_ok"],
            "tensor": ["xT4_pe", "q_pe", "kv_done", "ctx_tile_pe", "y_pe", "tr_pe", "a_pe", "t_pe", "u_pe", "low_pe",
                       "inter_pe", "rx_pe", "g_pe", "o_pe", "q2_pe", "k1_pe", "k2_pe", "q1_pe", "cum1_pe", "cum_pe", "sum_pe",
                       "den_pe", "og_pe", "bc_pe", "wo_pe", "v_pe"],
            "gpsimd": ["qm_ok", "am_ok", "vm_ok", "state_ok"],
        }
        for names in CREDITS.values():
            for name in names:
                S(name)

        def cur(n):
            return n + 2

        def prev(n):
            return n + 1

        def loads(n, p):
            return (n - p) * 8 + 16

        def wait_alone(eng, sem, value):
            eng.wait_ge(sem, value)
            eng.nop(nofuse=True)

        def whole(ap):
            return ap.rearrange("p a b -> p (a b)")

        def batches(eng):
            return eng.Fori(0, BATCH)

        block = ctx.enter_context(nc.Block())

        @block.sync
        def _(sp):
            def load_group(g):
                sp.dma_start(x4, x_g[bass.ds(g, 1), :, :, :].rearrange("a p t c -> (a p) t c")).then_inc(S("x4_in"), 16)

            def store_q(g):
                wait_alone(sp, S("q_read"), g * KT + KT + 1)
                for t in range(GT):
                    sp.dma_start(q_g[bass.ds(g, 1), t, :, :].rearrange("a p c -> (a p) c"),
                                 q4[:, t, :, :].rearrange("p a b -> p (a b)")).then_inc(S("q4_out"), 16)

            def load(j, p):
                sp.dma_start(xb[:, p, :], x_p[bass.ds(j, 1), p, :, :].rearrange("a p c -> (a p) c")).then_inc(S(f"xb{p}_in"), 16)
                sp.dma_start(qb[:, p, :, :].rearrange("p a b -> p (a b)"),
                             q_p[bass.ds(j, 1), p, :, :].rearrange("a p c -> (a p) c")).then_inc(S(f"qb{p}_in"), 16)

            def store(j, p):
                wait_alone(sp, S("out_ok"), cur(j * 2 + p))
                sp.dma_start(out_p[bass.ds(j, 1), p, :, :].rearrange("a p c -> (a p) c"), ob[:, p, :]).then_inc(S(f"out{p}"), 16)

            sp.dma_start(cst[:, :], consts_d).then_inc(S("consts_in"), 16)
            for k in range(KT):
                sp.dma_start(w_in[:, k, :], wqkv_d[:, k, :]).then_inc(S(f"wqkv{k}_in"), 16)
            for name in ("q4_out", "out0", "out1"):
                sp.sem_inc(S(name), 1)
            with batches(sp) as b:
                g0 = b * GROUPS
                wait_alone(sp, S("x1_ok"), b * TILES + 1)
                wait_alone(sp, S("qz_ok"), b * TILES + 1)
                load_group(g0)
                with sp.Fori(b * GROUPS, b * GROUPS + GROUPS - 1) as g:
                    wait_alone(sp, S("xf4_ok"), cur(g))
                    load_group(g + 1)
                    store_q(g)
                wait_alone(sp, S("xf4_ok"), cur(g0 + GROUPS - 1))
                store_q(g0 + GROUPS - 1)
                wait_alone(sp, S("q4_out"), (b + 1) * (16 * GT * GROUPS) + 1)
                j0 = b * (TILES // 2)
                for p in range(2):
                    load(j0, p)
                with sp.Fori(b * (TILES // 2) + 1, b * (TILES // 2) + TILES // 2) as j:
                    for p in range(2):
                        wait_alone(sp, S("x1_ok"), j * 2 + p)
                        wait_alone(sp, S("qz_ok"), j * 2 + p)
                        load(j, p)
                        store(j - 1, p)
            for p in range(2):
                wait_alone(sp, S(f"out{p}"), BATCH * (TILES // 2 * 16) + 1)

        @block.tensor
        def _(pe):
            mm = nc.tensor.matmul
            for name in CREDITS["tensor"]:
                pe.sem_inc(S(name), 1)
            pe.wait_ge(S("setup"), 1)

            def mm3(out, lhs, rhs, start, stop):
                mm(out, lhs(0), rhs(0), start=start, stop=False)
                mm(out, lhs(0), rhs(1), start=False, stop=False)
                return mm(out, lhs(1), rhs(0), start=False, stop=stop)

            def den(n, p, ahead):
                pe.wait_ge(S(f"qb{p}_in"), loads(n, p))
                if ahead:
                    pe.wait_ge(S("sil_ok"), prev(n))
                else:
                    pe.wait_ge(S("out_ok"), n + 1)
                for g in range(KT):
                    last = mm(bank[7][:, 0:P], kden[:, g, :], qb[:, p, g, :], start=(g == 0), stop=(g == KT - 1))
                last.then_inc(S("den_pe"), 1)

            def bc(n):
                pe.wait_ge(S("z_ok"), cur(n))
                pe.wait_ge(S("e2_ok"), prev(n))
                for g in range(KT):
                    last = mm(bank[6][:, g * P:(g + 1) * P], sel_bc[:, g, :], z[:, :], start=True, stop=True)
                last.then_inc(S("bc_pe"), 1)

            def y_mm(n):
                pe.wait_ge(S("qz_ok"), cur(n))
                pe.wait_ge(S("e1_ok"), prev(n))
                for g in range(KT):
                    last = mm(bank[5], qz[:, g, :], mix[:, g, :], start=(g == 0), stop=(g == KT - 1))
                last.then_inc(S("y_pe"), 1)

            def xn_transpose(n):
                pe.wait_ge(S("xn_ok"), cur(n))
                pe.wait_ge(S("exs_ok"), prev(n))
                for g in range(KT):
                    for part in range(2):
                        at = (part * KT + g) * P
                        last = nc.tensor.transpose(bank16[7][:, at:at + P], xn[:, part, g * P:(g + 1) * P], ident16[:, :])
                last.then_inc(S("t_pe"), 1)

            def low_rank(n):
                pe.wait_ge(S("xnT_ok"), cur(n))
                for part in range(2):
                    for g in range(KT):
                        mm3(bank[7][:, part * P:(part + 1) * P], lambda x: wl[:, x, g, part * P:(part + 1) * P],
                            lambda x: xnT[:, x, g, :], g == 0, g == KT - 1)
                for g in range(KT):
                    last = mm3(bank[7][:, 2 * P:2 * P + NEXP], lambda x: xnT[:, x, g, :], lambda x: wl[:, x, g, 2 * P:],
                               g == 0, g == KT - 1)
                last.then_inc(S("low_pe"), 1)

            def label_bc(n):
                pe.wait_ge(S("labi_ok"), cur(n))
                pe.wait_ge(S("am2_ok"), prev(n))
                mm(bank[0][:, 0:P], ones, lab_i[:, :], start=True, stop=True).then_inc(S("rx_pe"), 1)

            def second(out, which, k):
                return mm3(out, lambda x: low[:, x, which, :], lambda x: ws[:, x, k, :], True, True)

            def gates(n):
                pe.wait_ge(S("low_ok"), cur(n))
                pe.wait_ge(S("low0_ok"), cur(n))
                for k in range(3):
                    last = second(bank[5 + k], 0, k)
                last.then_inc(S("g_pe"), 1)

            def wide(n, where, w0, done):
                for g in range(KT):
                    last = mm3(bank[where], lambda x: xnT[:, x, g, :], lambda x: wb[:, x, g, w0:w0 + C], g == 0, g == KT - 1)
                last.then_inc(S(done), 1)

            def project_v(n):
                pe.wait_ge(S("carry_ok"), prev(n))
                wide(n, 1, 2 * C, "v_pe")

            def project_early(n):
                pe.wait_ge(S("mb_ok"), cur(n))
                second(bank[0], 1, 3).then_inc(S("q2_pe"), 1)
                wide(n, 2, C, "k1_pe")
                pe.wait_ge(S("v_ok"), cur(n))
                second(bank[1], 1, 4).then_inc(S("k2_pe"), 1)

            def cumulate(n):
                pe.wait_ge(S("ls_ok"), cur(n))
                pe.wait_ge(S("sil_ok"), cur(n))
                pe.wait_ge(S("same_ok"), cur(n))
                pe.wait_ge(S("hm_ok"), cur(n))
                mm(bank[5], centred, logsig[:, 0, :], start=True, stop=True).then_inc(S("cum1_pe"), 1)
                mm(bank[6], same_d[:, :], logsig[:, 1, :], start=True, stop=True).then_inc(S("cum_pe"), 1)

            def half_sums(n, ahead):
                if ahead:
                    pe.wait_ge(S("z_ok"), cur(n + 1))
                for pr in range(PAIRS):
                    f = slice(pr * P, (pr + 1) * P)
                    mm(bank[7][:, pr * 10:pr * 10 + 2], logsig[:, 0, f], halves, start=True, stop=True)
                    last = mm(bank[7][:, pr * 10 + 2:pr * 10 + 10], logsig[:, 1, f],
                              hm[:, :, :].rearrange("p e h -> p (e h)"), start=True, stop=True)
                last.then_inc(S("sum_pe"), 1)

            def transposes(n):
                for src, where, ready in ((q1g, 3, "q1g_ok"), (k1g, 2, "k1g_ok"), (q2g, 0, "q2g_ok"), (k2g, 1, "k2g_ok")):
                    pe.wait_ge(S(ready), cur(n))
                    for g in range(PAIRS):
                        last = nc.tensor.transpose(bank[where][:, g * P:(g + 1) * P], src[:, g * P:(g + 1) * P], ident)
                    last.then_inc(S("tr_pe"), 1)

            def scores(n, front):
                for kT, qT, where in ((k1T, q1T, (4, 5)), (k2T, q2T, (6, 0))):
                    if where[0] == 4:
                        if front:
                            pe.wait_ge(S("y_ok"), cur(n + 1))
                        pe.wait_ge(S("q1T_ok"), cur(n))
                        pe.wait_ge(S("k1T_ok"), cur(n))
                        pe.wait_ge(S("out_ok"), prev(n))
                    else:
                        pe.wait_ge(S("q2T_ok"), cur(n))
                        pe.wait_ge(S("k2T_ok"), cur(n))
                    for pr in range(PAIRS):
                        for odd in range(2):
                            h = slice(odd * D2, odd * D2 + D2)
                            last = mm(bank[where[odd]][:, pr * P:(pr + 1) * P], kT[h, pr, :], qT[h, pr, :], start=True, stop=True)
                    last.then_inc(S("a_pe"), 1)

            def state_products(n):
                pe.wait_ge(S("vm_ok"), cur(n))
                for pr in range(PAIRS):
                    mm(bank[1][:, pr * P:(pr + 1) * P], k1g[:, pr * P:(pr + 1) * P], v[:, pr * P:(pr + 1) * P], start=True, stop=True)
                for pr in range(PAIRS):
                    for odd in range(2):
                        h = 2 * pr + odd
                        last = mm(psum[odd * D2:odd * D2 + D2, 2 + pr // 2, (pr % 2) * 256:(pr % 2) * 256 + 256],
                                  k2g[:, h * D2:(h + 1) * D2], vm[:, :, h * D2:(h + 1) * D2], start=True, stop=True)
                last.then_inc(S("u_pe"), 1)

            def inter(n, pairs):
                if 0 in pairs:
                    pe.wait_ge(S("state_ok"), cur(n))
                    pe.wait_ge(S("am1_ok"), cur(n))
                    pe.wait_ge(S("qm_ok"), cur(n))
                for pr in pairs:
                    for path in range(PATHS):
                        q = q1T[:, pr, :] if path == 0 else qm[:, path - 1, pr, :]
                        last = mm(bank[4][:, pr * P:(pr + 1) * P], q, state[:, pr, path, :],
                                  start=(pr == 0 and path == 0), stop=False, skip_group_check=True)
                if PAIRS - 1 in pairs:
                    last.then_inc(S("inter_pe"), 1)

            def intra(n):
                pe.wait_ge(S("am_ok"), cur(n))
                for pr in range(PAIRS):
                    for odd in range(2):
                        h = 2 * pr + odd
                        last = mm(bank[4][:, h * D2:(h + 1) * D2], am1[:, odd, pr, :], v[:, h * D2:(h + 1) * D2],
                                  start=False, stop=True, skip_group_check=True)
                last.then_inc(S("o_pe"), 1)

            def og_transpose(n):
                pe.wait_ge(S("og_ok"), cur(n))
                for g in range(KT):
                    for part in range(2):
                        at = (part * KT + g) * P
                        last = nc.tensor.transpose(bank16[4][:, at:at + P], og16[:, part, g * P:(g + 1) * P], ident16[:, :])
                last.then_inc(S("og_pe"), 1)

            def out_mm(n):
                pe.wait_ge(S("ogT_ok"), cur(n))
                for g in range(KT):
                    last = mm3(bank[4], lambda x: ogT[:, x, g, :], lambda x: wo[:, x, g, :], g == 0, g == KT - 1)
                last.then_inc(S("wo_pe"), 1)

            def step(n, p, front=True, back=True, ahead=True):
                m = n - 1
                if front:
                    y_mm(n)
                if back:
                    transposes(m)
                    scores(m, front)
                    state_products(m)
                if front:
                    xn_transpose(n)
                if back:
                    inter(m, range(PAIRS // 2))
                if front:
                    low_rank(n)
                if back:
                    inter(m, range(PAIRS // 2, PAIRS))
                    intra(m)
                if front:
                    gates(n)
                    label_bc(n)
                    project_v(n)
                    project_early(n)
                if back:
                    og_transpose(m)
                if front:
                    wide(n, 3, 0, "q1_pe")
                if ahead:
                    den(n + 1, 1 - p, True)
                if front:
                    cumulate(n)
                if back:
                    out_mm(m)
                if ahead:
                    bc(n + 1)
                if front:
                    half_sums(n, ahead)

            with batches(pe) as b:
                def transpose4(g, tiles):
                    if tiles[0] == 0:
                        pe.wait_ge(S("xn4_ok"), cur(g))
                    for t in tiles:
                        pe.wait_ge(S("xT4_full"), g * GT + max(t, 1))
                        for k in range(KT):
                            for part in range(2):
                                at = (part * KT + k) * P
                                last = nc.tensor.transpose(bank16[t % 2][:, at:at + P], xn4[:, part, t, k * P:(k + 1) * P], ident16[:, :])
                        last.then_inc(S("xT4_pe"), 1)

                def context(g, t):
                    pe.wait_ge(S("kv0_full"), g * GT + t + 2)
                    pe.wait_ge(S("kv1_full"), g * GT + t + 2)
                    if t == 0:
                        pe.wait_ge(S("ctx_ok"), prev(g))
                    for h in range(KT):
                        last = mm(bank[6 + h // 2][:, (h % 2) * CTXW:(h % 2 + 1) * CTXW], kk[:, h * P:(h + 1) * P], vv[:, h, :],
                                  start=(t == 0 and h % 2 == 0), stop=(t == GT - 1), skip_group_check=True)
                    last.then_inc(S("ctx_tile_pe"), 1)

                def group(g, ahead=True):
                    transpose4(g, (2, 3))
                    pe.wait_ge(S("xT4_full"), g * GT + GT + 1)
                    pe.wait_ge(S("q_read"), g * KT + 1)
                    for m in range(KT):
                        if m >= 2:
                            pe.wait_ge(S("q_read"), g * KT + m)
                        for k in range(KT):
                            last = mm3(bank[2 + m % 2], lambda x: wqkv[:, x, k, m * P:(m + 1) * P], lambda x: xT4[:, x, k, :],
                                       k == 0, k == KT - 1)
                        last.then_inc(S("q_pe"), 1)
                    for t in range(GT):
                        for side in range(2):
                            pe.wait_ge(S(f"kv{side}_full"), g * GT + t + 1)
                            for k in range(KT):
                                last = mm3(bank[4 + side], lambda x: xT4[:, x, k, t * P:(t + 1) * P],
                                           lambda x: wqkv[:, x, k, C * (1 + side):C * (2 + side)], k == 0, k == KT - 1)
                            last.then_inc(S("kv_done"), 1)
                            if side == 0 and t > 0:
                                context(g, t - 1)
                    if ahead:
                        transpose4(g + 1, (0, 1))
                    context(g, GT - 1)

                g0 = b * GROUPS
                transpose4(g0, (0, 1))
                with pe.Fori(b * GROUPS, b * GROUPS + GROUPS - 1) as g:
                    group(g)
                group(g0 + GROUPS - 1, ahead=False)
                pe.wait_ge(S("ctx_blk_ok"), b + 1)
                for g in range(KT):
                    last = nc.tensor.transpose(bank[0][:, g * P:(g + 1) * P], ctx_blk[:, g, :], ident)
                last.then_inc(S("ctx_blk_pe"), 1)
                pe.wait_ge(S("ctxT_ok"), b + 1)
                pe.wait_ge(S("wproj_in"), b * 16 + 16)
                for g in range(KT):
                    mm(bank[1 + g], ctx_sum[:, g, 0:P], wproj[:, g, :], start=True, stop=True).then_inc(S("mix_pe"), 1)
                pe.wait_ge(S("mix_ok"), b + 1)
                n0 = b * TILES
                den(n0, 0, False)
                bc(n0)
                step(n0, 0, back=False)
                with pe.Fori(b * TILES + 1, b * TILES + TILES - 1, 2) as n:
                    step(n, 1)
                    step(n + 1, 0)
                step(n0 + TILES - 1, 1, ahead=False)
                step(n0 + TILES, 0, front=False, ahead=False)

        @block.scalar
        def _(act):
            ac = nc.scalar.activation
            act.add_instruction(mybir.InstLoadActFuncSet(name=nc.get_next_instruction_name(), act_func_set_id=ACT_SET_LN_EXP,
                                                         ins=[], outs=[]))
            for name in CREDITS["scalar"]:
                act.sem_inc(S(name), 1)
            for k in range(KT):
                act.wait_ge(S(f"wqkv{k}_in"), 16)
                ac(wqkv[:, 0, k, :], w_in[:, k, :], ACT.Copy, scale=W_SCALE).then_inc(S("wqkv_high"), 1)
            act.wait_ge(S("setup"), 1)

            def rstd_of(n, k, done_stat, eps=zero_eps):
                act.wait_ge(S(done_stat), n + 1)
                ac(lnv[:, k, :], mv[:, k, 1:2], ACT.Ln, bias=eps[:, :]).then_inc(S(f"lnv{k}_ok"), 1)
                act.wait_ge(S(f"lnv{k}_ok"), n + 1)
                ac(rstd[:, k, :], lnv[:, k, :], ACT.Exp, scale=-0.5).then_inc(S(f"rstd{k}"), 1)

            def to_cols(n, dst, where, k, done):
                act.wait_ge(S("tr_pe"), n * 4 + 2 + k)
                ac(dst.rearrange("p a b -> p (a b)"), bank[where], ACT.Copy).then_inc(S(done), 1)

            def front_norm1(n):
                rstd_of(n, 0, "mv0_ok")

            def front_norm2(n):
                rstd_of(n, 1, "mv1_ok")

            def front_low(n):
                act.wait_ge(S("t_pe"), cur(n))
                act.wait_ge(S("q1_pe"), prev(n))
                ac(xnT.rearrange("p x a b -> p (x a b)"), bank16[7], ACT.Copy).then_inc(S("xnT_ok"), 1)
                act.wait_ge(S("low_pe"), cur(n))
                act.wait_ge(S("low_ok"), prev(n))
                ac(lowf[:, 0, :], bank[7][:, 0:P], ACT.Identity, bias=one_rows, scale=1.0 / (W_SCALE * S_SCALE))
                ac(lowf[:, 1, :], bank[7][:, P:2 * P], ACT.Copy, scale=1.0 / (W_SCALE * S_SCALE)).then_inc(S("low1_ok"), 1)
                ac(logit_s, bank[7][:, 2 * P:2 * P + NEXP], ACT.Copy, scale=1.0 / W_SCALE).then_inc(S("low0_ok"), 1)
                act.wait_ge(S("ldiff_ok"), n + 1)
                ac(lexp[:, :], ldiff[:, :], ACT.Exp, accum_out=lsum[:, :]).then_inc(S("lexp_ok"), 1)

            def front_gates(n, part):
                if part == 1:
                    act.wait_ge(S("ex_ok"), cur(n))
                    ac(gch, gch, ACT.Ln, bias=1.0).then_inc(S("ln_ok"), 1)
                    return
                act.wait_ge(S("g_pe"), cur(n))
                act.wait_ge(S("ls_ok"), prev(n))
                ac(gch, psum[:, 5:8, :].rearrange("p a b -> p (a b)"), ACT.Abs).then_inc(S("abs_ok"), 1)
                act.wait_ge(S("abs_ok"), cur(n))
                ac(gch, gch, ACT.Exp, scale=-1.0).then_inc(S("ex_ok"), 1)

            def front_sig(n):
                act.wait_ge(S("ls_ok"), cur(n))
                ac(logsig[:, 2, :], logsig[:, 2, :], ACT.Exp).then_inc(S("sig_ok"), 1)

            def front_v(n):
                act.wait_ge(S("v_pe"), cur(n))
                act.wait_ge(S("vm_ok"), prev(n))
                ac(v, bank[1], ACT.Copy, scale=1.0 / W_SCALE).then_inc(S("v_ok"), 1)

            def front_ke(n):
                act.wait_ge(S("kd_ok"), cur(n))
                ac(kd, kd, ACT.Exp).then_inc(S("ke_ok"), 1)

            def front_exps(n):
                act.wait_ge(S("cum1_pe"), cur(n))
                act.wait_ge(S("tr_pe"), n * 4 + 1)
                act.wait_ge(S("u_pe"), prev(n))
                ac(ep1, bank[5], ACT.Exp)
                ac(em1, bank[5], ACT.Exp, scale=-1.0).then_inc(S("e1_ok"), 1)
                act.wait_ge(S("cum_pe"), cur(n))
                ac(ep2, bank[6], ACT.Exp)
                ac(em2, bank[6], ACT.Exp, scale=-1.0).then_inc(S("e2_ok"), 1)

            def front_exs(n, p):
                act.wait_ge(S("sum_pe"), cur(n))
                act.wait_ge(S("state_ok"), prev(n))
                ac(exs[:, p, :, :, :].rearrange("p a b c -> p (a b c)"), bank[7][:, 0:PAIRS * 10], ACT.Exp).then_inc(S("exs_ok"), 1)

            def back_transposed(n):
                act.wait_ge(S("inter_pe"), prev(n))
                to_cols(n, q1T, 3, 0, "q1T_ok")
                act.wait_ge(S("a_pe"), n * 2 + 1)
                to_cols(n, k1T, 2, 1, "k1T_ok")

            def back_transposed2(n):
                act.wait_ge(S("qm_ok"), prev(n))
                to_cols(n, q2T, 0, 2, "q2T_ok")
                to_cols(n, k2T, 1, 3, "k2T_ok")

            def back_square(n):
                act.wait_ge(S("o_pe"), cur(n))
                act.wait_ge(S("og_ok"), prev(n))
                ac(osq[:, :], bank[4], ACT.Square).then_inc(S("osq_ok"), 1)

            def back_rms(n):
                act.wait_ge(S("oms_ok"), n + 2)
                ac(oln[:, :], oms[:, :], ACT.Ln, bias=zero_eps[:, :], scale=1.0 / D2).then_inc(S("oln_ok"), 1)
                act.wait_ge(S("oln_ok"), n + 1)
                ac(ors[:, :], oln[:, :], ACT.Exp, scale=-0.5).then_inc(S("ors_ok"), 1)

            def back_og(n):
                act.wait_ge(S("og_pe"), cur(n))
                act.wait_ge(S("wo_pe"), prev(n))
                ac(ogT[:, :, :, :].rearrange("p x a b -> p (x a b)"), bank16[4], ACT.Copy).then_inc(S("ogT_ok"), 1)

            def back_norm3(n):
                rstd_of(n, 2, "mv2_ok", eps_scaled)

            def step(n, p, front=True, back=True):
                m = n - 1
                if back:
                    back_transposed(m)
                    back_transposed2(m)
                if front:
                    front_norm1(n)
                    front_norm2(n)
                if front:
                    front_low(n)
                if back:
                    back_square(m)
                if front:
                    front_gates(n, 0)
                if back:
                    back_rms(m)
                if front:
                    front_gates(n, 1)
                    front_v(n)
                    front_sig(n)
                    front_ke(n)
                if back:
                    back_og(m)
                if front:
                    front_exps(n)
                    front_exs(n, p)
                if back:
                    back_norm3(m)

            with batches(act) as b:
                def norm4(g):
                    act.wait_ge(S("mv1_all"), g + 1)
                    ac(lnv1[:, :, :], mv1[:, :, 1:2], ACT.Ln, bias=zero_eps[:, :]).then_inc(S("lnv_all"), 1)
                    act.wait_ge(S("lnv_all"), g + 1)
                    ac(rstd1[:, :, :], lnv1[:, :, :], ACT.Exp, scale=-0.5).then_inc(S("rstd1_all"), 1)

                def full4(g, tiles):
                    act.wait_ge(S("kv_done"), g * (2 * GT) + 1)
                    for t in tiles:
                        act.wait_ge(S("xT4_pe"), g * GT + t + 2)
                        ac(xT4[:, :, :, t * P:(t + 1) * P].rearrange("p x k c -> p (x k) c"),
                           bank16[t % 2].rearrange("p (k c) -> p k c", k=2 * KT), ACT.Copy).then_inc(S("xT4_full"), 1)

                def group(g, ahead=True):
                    full4(g, (2, 3))
                    act.wait_ge(S("q4_out"), g * (16 * GT) + 1)
                    for m in range(KT):
                        act.wait_ge(S("q_pe"), g * KT + m + 2)
                        ac(q4[:, :, m, :], bank[2 + m % 2].rearrange("p (t c) -> p t c", t=GT), ACT.Relu,
                           scale=1.0 / W_SCALE).then_inc(S("q_read"), 1)
                    if ahead:
                        norm4(g + 1)
                    for t in range(GT):
                        act.wait_ge(S("kv_done"), 2 * (g * GT + t) + 2)
                        act.wait_ge(S("ctx_tile_pe"), g * GT + t + 1)
                        ac(kk, bank[4], ACT.Relu, scale=1.0 / W_SCALE).then_inc(S("kv0_full"), 1)
                        act.wait_ge(S("kv_done"), 2 * (g * GT + t) + 3)
                        ac(vv[:, :, 0:P], bank[5].rearrange("p (k c) -> p k c", k=KT), ACT.Copy,
                           scale=1.0 / W_SCALE).then_inc(S("kv1_full"), 1)
                    if ahead:
                        full4(g + 1, (0, 1))

                g0 = b * GROUPS
                norm4(g0)
                full4(g0, (0, 1))
                with act.Fori(b * GROUPS, b * GROUPS + GROUPS - 1) as g:
                    group(g)
                group(g0 + GROUPS - 1, ahead=False)
                act.wait_ge(S("ctx_blk_pe"), b + 1)
                ac(ctx_sum[:, :, 0:P], bank[0].rearrange("p (k c) -> p k c", k=KT), ACT.Copy).then_inc(S("ctxT_ok"), 1)
                for g in range(KT):
                    act.wait_ge(S("mix_pe"), b * KT + g + 1)
                    last = ac(mix[:, g, :], bank[1 + g], ACT.Copy)
                last.then_inc(S("mix_ok"), 1)
                n0 = b * TILES
                step(n0, 0, back=False)
                with act.Fori(b * TILES + 1, b * TILES + TILES - 1, 2) as n:
                    step(n, 1)
                    step(n + 1, 0)
                step(n0 + TILES - 1, 1)
                step(n0 + TILES, 0, front=False)
                for p in range(2):
                    wait_alone(act, S("out_ok"), cur(n0 + TILES - 2 + p))
                    act.dma_start(out_p[bass.ds((b + 1) * (TILES // 2) - 1, 1), p, :, :].rearrange("a p c -> (a p) c"),
                                   ob[:, p, :]).then_inc(S(f"out{p}"), 16)

        @block.gpsimd
        def _(pool):
            for name in CREDITS["gpsimd"]:
                pool.sem_inc(S(name), 1)
            pool.wait_ge(S("setup"), 1)
            pool.nop(nofuse=True)
            for dst, src in ((bproj[:, :], bproj_d), (nw[:, :], nw_d), (wb_in, whole(wb_d)),
                             (wl_in, whole(wl_d)), (ws_in, whole(ws_d)), (wo_in, whole(wo_d))):
                pool.dma_start(dst, src).then_inc(S("weights_in"), 16)
            pool.wait_ge(S("weights_in"), 16 * 6)
            late = ((wb_in, wb, W_SCALE, 1.0), (wl_in, wl, W_SCALE, 1.0), (ws_in, ws, S_SCALE, 1.0), (wo_in, wo, W_SCALE, nw[:, :]))
            for src, dst, scale, by in late:
                last = nc.gpsimd.tensor_scalar(src, src, by, scale, ALU.mult, ALU.mult)
            last.then_inc(S("late_scaled"), 1)
            pool.wait_ge(S("late_scaled"), 1)
            for src, dst, scale, by in late:
                last = nc.gpsimd.tensor_scalar(dst[:, 0, :, :].rearrange("p a b -> p (a b)"), src, 1.0, 1.0, ALU.mult, ALU.mult)
            last.then_inc(S("late_high"), 1)
            pool.wait_ge(S("late_high"), 1)
            for src, dst, scale, by in late:
                last = nc.gpsimd.tensor_tensor(dst[:, 1, :, :].rearrange("p a b -> p (a b)"), src,
                                               dst[:, 0, :, :].rearrange("p a b -> p (a b)"), ALU.subtract)
            last.then_inc(S("late_split"), 1)

            def back_qm(n):
                pool.wait_ge(S("q2T_ok"), cur(n))
                pool.wait_ge(S("mb_ok"), cur(n))
                pool.wait_ge(S("state_ok"), cur(n))
                pool.wait_ge(S("inter_pe"), prev(n))
                for e in range(NEXP):
                    last = nc.gpsimd.tensor_tensor(qm[:, e, :, :], q2T, mb[:, e, :].unsqueeze(1).to_broadcast([P, PAIRS, P]), ALU.mult)
                last.then_inc(S("qm_ok"), 1)

            def back_am(n):
                pool.wait_ge(S("am2_ok"), cur(n))
                pool.wait_ge(S("am1_ok"), cur(n))
                nc.gpsimd.tensor_tensor(am1[:, :, :, :], am1[:, :, :, :], am2[:, :, :, :], ALU.add).then_inc(S("am_ok"), 1)

            def front_vm(n):
                pool.wait_ge(S("v_ok"), cur(n))
                pool.wait_ge(S("hm_ok"), cur(n))
                wait_alone(pool, S("u_pe"), prev(n))
                for e in range(NEXP):
                    last = nc.gpsimd.tensor_scalar(vm[:, e, :], v, m4[:, e:e + 1], 1.0, ALU.mult, ALU.mult)
                last.then_inc(S("vm_ok"), 1)

            def front_state(n):
                pool.wait_ge(S("decay_ok"), n + 1)
                pool.wait_ge(S("inter_pe"), prev(n))
                pool.wait_ge(S("carry_ok"), prev(n))
                pool.wait_ge(S("vm_ok"), cur(n))
                for odd, done in ((0, "state_half"), (1, "state_ok")):
                    h = slice(odd * D2, odd * D2 + D2)
                    if odd:
                        pool.wait_ge(S("state_half"), n + 1)
                    nc.gpsimd.tensor_tensor(state[h, :, :, h], carry[h, :, :, :],
                                            decay[h, :, :].unsqueeze(3).to_broadcast([D2, PAIRS, PATHS, D2]),
                                            ALU.mult).then_inc(S(done), 1)

            def step(n, p, front=True, back=True):
                if back:
                    back_qm(n - 1)
                    back_am(n - 1)
                if front:
                    front_vm(n)
                    front_state(n)

            pool.wait_ge(S("late_split"), 1)
            with batches(pool) as b:
                wait_alone(pool, S("out_ok"), b * TILES + 1)
                pool.dma_start(wproj, wproj_d).then_inc(S("wproj_in"), 16)
                n0 = b * TILES
                step(n0, 0, back=False)
                with pool.Fori(b * TILES + 1, b * TILES + TILES - 1, 2) as n:
                    step(n, 1)
                    step(n + 1, 0)
                step(n0 + TILES - 1, 1)
                step(n0 + TILES, 0, front=False)

        @block.vector
        def _(dve):
            ve = nc.vector
            for name in CREDITS["vector"] + ["oms_ok"]:
                dve.sem_inc(S(name), 1)
            ve.memset(zero_eps[:, :], EPS)
            ve.memset(eps_scaled[:, :], EPS * W_SCALE * W_SCALE)
            ve.memset(z[:, :], 0.0)
            ve.memset(exs[:, :, :, :, :], 1.0)
            ve.memset(mv[:, :, :], 1.0)
            dve.wait_ge(S("consts_in"), 16)
            ve.tensor_copy(ident16[:, :], ident)
            for k in range(KT):
                dve.wait_ge(S(f"wqkv{k}_in"), 16)
                dve.wait_ge(S("wqkv_high"), k + 1)
                last = ve.scalar_tensor_tensor(wqkv[:, 1, k, :], w_in[:, k, :], W_SCALE, wqkv[:, 0, k, :], ALU.mult, ALU.subtract)
            last.then_inc(S("setup"), 1)

            def flat(ap):
                return ap.rearrange("p a b -> p (a b)")

            def heads(ap):
                return ap.rearrange("p (h d) -> p h d", h=H2)

            def wide(ap, n):
                return ap.unsqueeze(2).to_broadcast([ap.shape[0], ap.shape[1], n])

            def stats(n, k, src):
                ve.bn_stats(st[:, k, :], src).then_inc(S(f"st{k}_ok"), 1)
                wait_alone(dve, S(f"st{k}_ok"), n + 1)
                ve.bn_aggr(mv[:, k, :], st[:, k, :]).then_inc(S(f"mv{k}_ok"), 1)

            def normed(n, k, dst, src, done, value):
                dve.wait_ge(S(f"rstd{k}"), n + 1)
                ve.tensor_scalar(dst, src, mv[:, k, 0:1], rstd[:, k, :], ALU.subtract, ALU.mult).then_inc(S(done), 1)
                dve.wait_ge(S(done), value)

            def split(n, dst, src, high, done):
                ve.tensor_copy(dst[:, 0], src).then_inc(S(high), 1)
                dve.wait_ge(S(high), n + 1)
                ve.tensor_tensor(dst[:, 1], src, dst[:, 0], ALU.subtract).then_inc(S(done), 1)

            def front_norms(n, p):
                dve.wait_ge(S("y_pe"), cur(n))
                ve.tensor_tensor(y, bank[5], bproj[:, :], ALU.add).then_inc(S("y_ok"), 1)
                dve.wait_ge(S("y_ok"), cur(n))
                stats(n, 0, y)
                normed(n, 0, y, y, "yn_ok", n + 1)
                dve.wait_ge(S(f"xb{p}_in"), loads(n, p))
                ve.tensor_tensor(x1[:, p, :], xb[:, p, :], y, ALU.add).then_inc(S("x1_ok"), 1)
                dve.wait_ge(S("x1_ok"), cur(n))
                stats(n, 1, x1[:, p, :])
                dve.wait_ge(S("t_pe"), prev(n))
                normed(n, 1, xnf, x1[:, p, :], "xnf_ok", n + 1)
                split(n, xn, xnf, "xnh_ok", "xn_ok")

            def back_masks(n):
                dve.wait_ge(S("a_pe"), n * 2 + 2)
                dve.wait_ge(S("o_pe"), prev(n))
                for odd in range(2):
                    last = ve.tensor_tensor(am1[:, odd, :, :], bank[4 + odd].rearrange("p (a b) -> p a b", a=PAIRS),
                                            causal.unsqueeze(1).to_broadcast([P, PAIRS, P]), ALU.mult)
                last.then_inc(S("am1_ok"), 1)
                dve.wait_ge(S("a_pe"), n * 2 + 3)
                dve.wait_ge(S("am_ok"), prev(n))
                for odd in range(2):
                    last = ve.tensor_tensor(am2[:, odd, :, :], bank[(6, 0)[odd]].rearrange("p (a b) -> p a b", a=PAIRS),
                                            same_c[:, :].unsqueeze(1).to_broadcast([P, PAIRS, P]), ALU.mult)
                last.then_inc(S("am2_ok"), 1)

            def back_carry(n):
                dve.wait_ge(S("u_pe"), cur(n))
                dve.wait_ge(S("state_ok"), cur(n))
                for odd in range(2):
                    h = slice(odd * D2, odd * D2 + D2)
                    ve.tensor_tensor(carry[h, :, 0, :], bank[1][h, :].rearrange("p (a b) -> p a b", a=PAIRS)[:, :, h],
                                     state[h, :, 0, h], ALU.add)
                    last = ve.tensor_tensor(carry[h, :, 1:PATHS, :], psum[h, 2:4, :].rearrange("p a (r e d) -> p (a r) e d", r=2, e=NEXP),
                                            state[h, :, 1:PATHS, h], ALU.add)
                last.then_inc(S("carry_ok"), 1)

            def front_low(n):
                dve.wait_ge(S("low1_ok"), cur(n))
                dve.wait_ge(S("k2_pe"), prev(n))
                split(n, low, lowf, "lowh_ok", "low_ok")

            def front_router(n):
                dve.wait_ge(S("low0_ok"), cur(n))
                ve.reduce_max(lmax[:, :], logit_s, X).then_inc(S("lmax_ok"), 1)
                dve.wait_ge(S("lmax_ok"), n + 1)
                ve.tensor_scalar(ldiff[:, :], logit_s, lmax[:, :], None, ALU.subtract).then_inc(S("ldiff_ok"), 1)
                dve.wait_ge(S("ldiff_ok"), n + 1)
                ve.scalar_tensor_tensor(lscore[:, :], ldiff[:, :], 0.0, score, ALU.is_equal, ALU.mult).then_inc(S("lscore_ok"), 1)
                dve.wait_ge(S("lscore_ok"), n + 1)
                ve.reduce_max(lab[:, :], lscore[:, :], X).then_inc(S("lab_ok"), 1)
                dve.wait_ge(S("lab_ok"), n + 1)
                dve.wait_ge(S("rx_pe"), prev(n))
                ve.tensor_scalar(lab_i[:, :], ident, lab[:, :], None, ALU.mult).then_inc(S("labi_ok"), 1)
                dve.wait_ge(S("vm_ok"), prev(n))
                ve.tensor_scalar(m4[:, :], score, lab[:, :], None, ALU.is_equal).then_inc(S("m4_ok"), 1)
                dve.wait_ge(S("m4_ok"), n + 1)
                dve.wait_ge(S("sum_pe"), prev(n))
                ve.tensor_tensor(hm[:, :, :], wide(m4[:, :], 2), halves.unsqueeze(1).to_broadcast([P, NEXP, 2]), ALU.mult).then_inc(S("hm_ok"), 1)
                dve.wait_ge(S("lexp_ok"), cur(n))
                ve.reciprocal(rr[:, :], lsum[:, :]).then_inc(S("rr_ok"), 1)
                dve.wait_ge(S("rr_ok"), n + 1)
                ve.tensor_scalar(rq[:, :], rr[:, :], D2 ** -0.5, None, ALU.mult).then_inc(S("rq_ok"), 1)

            def front_masks(n):
                dve.wait_ge(S("rx_pe"), cur(n))
                dve.wait_ge(S("cum_pe"), prev(n))
                row = bank[0][:, 0:P]
                ve.scalar_tensor_tensor(same_d[:, :], row, lab[:, :], centred, ALU.is_equal, ALU.mult)
                ve.scalar_tensor_tensor(same_c[:, :], row, lab[:, :], causal, ALU.is_equal, ALU.mult).then_inc(S("same_ok"), 1)
                dve.wait_ge(S("qm_ok"), prev(n))
                for e in range(NEXP):
                    last = ve.tensor_scalar(mb[:, e, :], row, float(NEXP - e), None, ALU.is_equal)
                last.then_inc(S("mb_ok"), 1)

            def front_logsig(n):
                dve.wait_ge(S("ln_ok"), cur(n))
                dve.wait_ge(S("sum_pe"), prev(n))
                dve.wait_ge(S("sil_ok"), prev(n))
                ve.scalar_tensor_tensor(flat(logsig), psum[:, 5:8, :].rearrange("p a b -> p (a b)"), 0.0, gch,
                                        ALU.min, ALU.subtract).then_inc(S("ls_ok"), 1)

            def front_sil(n, p):
                dve.wait_ge(S("sig_ok"), cur(n))
                ve.tensor_tensor(sil[:, p, :], bank[7], logsig[:, 2, :], ALU.mult).then_inc(S("sil_ok"), 1)

            def front_softmax(n):
                dve.wait_ge(S("k2_pe"), cur(n))
                ve.reduce_max(kmax[:, :], heads(bank[1]), X).then_inc(S("kmax_ok"), 1)
                dve.wait_ge(S("kmax_ok"), n + 1)
                dve.wait_ge(S("kr_ok"), prev(n))
                dve.wait_ge(S("k2g_ok"), prev(n))
                ve.tensor_tensor(heads(kd), heads(bank[1]), wide(kmax[:, :], D2), ALU.subtract).then_inc(S("kd_ok"), 1)
                dve.wait_ge(S("ke_ok"), cur(n))
                ve.reduce_sum(ksum[:, :], heads(kd), X).then_inc(S("ksum_ok"), 1)
                dve.wait_ge(S("ksum_ok"), n + 1)
                ve.reciprocal(krec[:, :], ksum[:, :]).then_inc(S("krec_ok"), 1)
                dve.wait_ge(S("krec_ok"), n + 1)
                ve.tensor_scalar(kfac[:, :], krec[:, :], rr[:, :], None, ALU.mult).then_inc(S("kfac_ok"), 1)
                dve.wait_ge(S("kfac_ok"), n + 1)
                ve.tensor_tensor(heads(kd), heads(kd), wide(kfac[:, :], D2), ALU.mult).then_inc(S("kr_ok"), 1)

            def front_gated(n):
                dve.wait_ge(S("e1_ok"), cur(n))
                dve.wait_ge(S("q1_pe"), cur(n))
                ve.scalar_tensor_tensor(q1g, bank[3], D2 ** -0.5 / W_SCALE, ep1, ALU.mult, ALU.mult).then_inc(S("q1g_ok"), 1)
                ve.scalar_tensor_tensor(k1g, bank[2], 1.0 / W_SCALE, em1, ALU.mult, ALU.mult).then_inc(S("k1g_ok"), 1)
                dve.wait_ge(S("e2_ok"), cur(n))
                dve.wait_ge(S("rq_ok"), n + 1)
                ve.scalar_tensor_tensor(q2g, bank[0], rq[:, :], ep2, ALU.mult, ALU.mult).then_inc(S("q2g_ok"), 1)
                dve.wait_ge(S("kr_ok"), cur(n))
                ve.tensor_tensor(k2g, kd, em2, ALU.mult).then_inc(S("k2g_ok"), 1)

            def front_decay(n, p):
                dve.wait_ge(S("exs_ok"), cur(n))
                dve.wait_ge(S("state_ok"), prev(n))
                ve.tensor_tensor(decay[:, :, :], exs[:, 1 - p, :, :, 1], exs[:, p, :, :, 0], ALU.mult).then_inc(S("decay_ok"), 1)

            def ahead_z(n):
                dve.wait_ge(S("den_pe"), cur(n))
                dve.wait_ge(S("bc_pe"), prev(n))
                ve.tensor_scalar(z[0:H1, :], bank[7][0:H1, 0:P], EPS_Z, None, ALU.add).then_inc(S("zd_ok"), 1)
                dve.wait_ge(S("zd_ok"), n + 1)
                ve.reciprocal(z[0:H1, :], z[0:H1, :]).then_inc(S("z_ok"), 1)

            def ahead_qz(n, p):
                dve.wait_ge(S("bc_pe"), cur(n))
                dve.wait_ge(S("y_pe"), prev(n))
                ve.tensor_tensor(flat(qz), bank[6], flat(qb[:, p, :, :]), ALU.mult).then_inc(S("qz_ok"), 1)

            def back_norm(n):
                dve.wait_ge(S("osq_ok"), cur(n))
                ve.reduce_sum(oms[:, :], heads(osq[:, :]), X).then_inc(S("oms_ok"), 1)

            def back_normed(n, p):
                dve.wait_ge(S("ors_ok"), n + 1)
                ve.tensor_tensor(heads(og[:, :]), heads(bank[4]), wide(ors[:, :], D2), ALU.mult).then_inc(S("on_ok"), 1)
                dve.wait_ge(S("on_ok"), cur(n))
                ve.tensor_tensor(og[:, :], og[:, :], sil[:, p, :], ALU.mult).then_inc(S("ogf_ok"), 1)
                dve.wait_ge(S("ogf_ok"), n + 1)
                dve.wait_ge(S("og_pe"), prev(n))
                split(n, og16[:, :, :], og[:, :], "ogh_ok", "og_ok")

            def back_stats(n):
                dve.wait_ge(S("wo_pe"), cur(n))
                stats(n, 2, bank[4])

            def back_out(n, p):
                dve.wait_ge(S(f"out{p}"), (n - p) * 8 + 1)
                normed(n, 2, ob[:, p, :], bank[4], "obn_ok", n + 1)
                ve.tensor_tensor(ob[:, p, :], ob[:, p, :], x1[:, p, :], ALU.add).then_inc(S("out_ok"), 1)

            def step(n, p, front=True, back=True, ahead=True):
                m, mp = n - 1, 1 - p
                if front:
                    front_norms(n, p)
                if back:
                    back_masks(m)
                    back_carry(m)
                if front:
                    front_low(n)
                    front_router(n)
                if back:
                    back_norm(m)
                if front:
                    front_masks(n)
                if back:
                    back_normed(m, mp)
                if front:
                    front_logsig(n)
                    front_sil(n, p)
                    front_softmax(n)
                if ahead:
                    ahead_z(n + 1)
                if front:
                    front_gated(n)
                if ahead:
                    ahead_qz(n + 1, mp)
                if back:
                    back_stats(m)
                if front:
                    front_decay(n, p)
                if back:
                    back_out(m, mp)

            dve.wait_ge(S("setup"), 1)
            with batches(dve) as b:
                dve.wait_ge(S("out_ok"), b * TILES + 1)
                ve.memset(vv[:, :, P:CTXW], 1.0)
                ve.memset(ctx_sum[:, :, :], 0.0).then_inc(S("ctx_zero"), 1)
                dve.wait_ge(S("ctx_zero"), b + 1)
                def norm4(g):
                    dve.wait_ge(S("x4_in"), g * 16 + 16)
                    for t in range(GT):
                        last = ve.bn_stats(st1[:, t, :], x4[:, t, :])
                    last.then_inc(S("st1_all"), 1)
                    wait_alone(dve, S("st1_all"), g + 1)
                    for t in range(GT):
                        last = ve.bn_aggr(mv1[:, t, :], st1[:, t, :])
                    last.then_inc(S("mv1_all"), 1)
                    dve.wait_ge(S("rstd1_all"), g + 1)
                    for t in range(GT):
                        last = ve.tensor_scalar(xf4[:, t, :], x4[:, t, :], mv1[:, t, 0:1], rstd1[:, t, :], ALU.subtract, ALU.mult)
                    last.then_inc(S("xf4_ok"), 1)
                    dve.wait_ge(S("xf4_ok"), cur(g))
                    dve.wait_ge(S("xT4_pe"), g * GT + 1)
                    ve.tensor_copy(flat(xn4[:, 0]), flat(xf4)).then_inc(S("xh4_ok"), 1)
                    dve.wait_ge(S("xh4_ok"), g + 1)
                    ve.tensor_tensor(flat(xn4[:, 1]), flat(xf4), flat(xn4[:, 0]), ALU.subtract).then_inc(S("xn4_ok"), 1)

                def add_context(g):
                    dve.wait_ge(S("ctx_tile_pe"), g * GT + GT + 1)
                    for k in range(2):
                        last = ve.tensor_tensor(ctx_sum[:, 2 * k:2 * k + 2, :],
                                                bank[6 + k][:, 0:2 * CTXW].rearrange("p (a b) -> p a b", a=2),
                                                ctx_sum[:, 2 * k:2 * k + 2, :], ALU.add)
                    last.then_inc(S("ctx_ok"), 1)

                g0 = b * GROUPS
                norm4(g0)
                with dve.Fori(b * GROUPS, b * GROUPS + GROUPS - 1) as g:
                    norm4(g + 1)
                    add_context(g)
                    dve.wait_ge(S("ctx_ok"), cur(g))
                add_context(g0 + GROUPS - 1)
                dve.wait_ge(S("ctx_ok"), cur(g0 + GROUPS - 1))
                ve.tensor_tensor(kden[:, :, :], sel_den, ctx_sum[:, :, P:CTXW].to_broadcast([P, KT, P]), ALU.mult)
                ve.tensor_tensor(ctx_blk[:, :, :], ctx_sum[:, :, 0:P], blocks.unsqueeze(1).to_broadcast([P, KT, P]), ALU.mult)\
                    .then_inc(S("ctx_blk_ok"), 1)
                dve.wait_ge(S("late_split"), 1)
                ve.memset(state, 0.0)
                ve.memset(carry, 0.0).then_inc(S("carry_zero"), 1)
                dve.wait_ge(S("carry_zero"), b + 1)
                dve.wait_ge(S("ctxT_ok"), b + 1)
                n0 = b * TILES
                ahead_z(n0)
                ahead_qz(n0, 0)
                step(n0, 0, back=False)
                with dve.Fori(b * TILES + 1, b * TILES + TILES - 1, 2) as n:
                    step(n, 1)
                    step(n + 1, 0)
                step(n0 + TILES - 1, 1, ahead=False)
                step(n0 + TILES, 0, front=False, ahead=False)


def layouts(i):
    import numpy as np

    def tiles(w):
        return np.ascontiguousarray(w.reshape(w.shape[0] // P, P, w.shape[1]).transpose(1, 0, 2))

    a = {k: np.asarray(v) for k, v in i.items()}
    low = np.zeros((C, L_COLS), np.float32)
    low[:, 0:LORA] = a["L0_ffn_Wga"]
    low[:, ROW_G1:ROW_G1 + GLR] = a["L0_ffn_Wg1a"]
    low[:, ROW_G2:ROW_G2 + GLR] = a["L0_ffn_Wg2a"]
    low[:, P:P + LORA] = a["L0_ffn_Wqa"]
    low[:, P + LORA:2 * P] = a["L0_ffn_Wka"]
    low[:, 2 * P:] = a["L0_ffn_We"]
    second = np.zeros((P, 5, C), np.float32)
    second[ROW_G1:ROW_G1 + GLR, 0] = a["L0_ffn_Wg1b"]
    second[ROW_G1 + GLR, 0] = a["L0_ffn_bg1"]
    second[ROW_G2:ROW_G2 + GLR, 1] = a["L0_ffn_Wg2b"]
    second[ROW_G2 + GLR, 1] = a["L0_ffn_bg2"]
    second[0:LORA, 2] = a["L0_ffn_Wgb"]
    second[0:LORA, 3] = a["L0_ffn_Wqb"]
    second[LORA:, 4] = a["L0_ffn_Wkb"]
    cst = np.zeros((P, N_CONSTS), np.float32)
    s, t = np.arange(P)[:, None], np.arange(P)[None, :]

    def put(name, value):
        lo, hi = CONSTS[name]
        cst[:value.shape[0], lo:hi] = value

    put("ident", np.eye(P))
    put("causal", t >= s)
    put("centred", (1.0 * (t >= s) - 1.0 * (s < HALF)) / NORMALIZER)
    put("halves", np.concatenate([s < HALF, s >= HALF], 1) / NORMALIZER)
    put("blocks", s // D1 == t // D1)
    head = np.arange(KT)[:, None] * (P // D1) + np.arange(P)[None, :] // D1
    sel = np.arange(P)[:, None, None] == head[None]
    put("sel_bc", sel.reshape(P, KT * P))
    put("sel_den", sel.transpose(2, 1, 0).reshape(P, KT * P))
    put("score", np.broadcast_to(np.arange(NEXP, 0, -1)[None], (P, NEXP)))
    put("one_rows", ((s == ROW_G1 + GLR) | (s == ROW_G2 + GLR)) / S_SCALE)
    put("ones", np.ones((P, P)))
    return {
        "x": np.ascontiguousarray(a["L0_attn_x"].reshape(BATCH * SEQ, C)),
        "wqkv": tiles(a["L0_attn_w_qkv"].T),
        "wproj": tiles(a["L0_attn_w_proj"].T),
        "bproj": np.ascontiguousarray(np.broadcast_to(a["L0_attn_b_proj"][None], (P, C))),
        "wb": tiles(np.concatenate([a["L0_ffn_Wq"], a["L0_ffn_Wk"], a["L0_ffn_Wv"]], 1)),
        "wl": tiles(low),
        "ws": second,
        "wo": tiles(a["L0_ffn_Wo"]),
        "nw": np.ascontiguousarray(np.tile(a["L0_ffn_norm_w"], 2)[:, None]),
        "consts": cst,
    }


def kernel(**inputs):
    import numpy as np
    import concourse.bacc as bacc
    from concourse.bass_utils import run_bass_kernel_spmd

    nc = bacc.Bacc("TRN2", target_bir_lowering=False, num_devices=1)
    arrays = layouts(inputs)
    args = [nc.dram_tensor(f"{n}_in", a.shape, mybir.dt.from_np(a.dtype), kind="ExternalInput").ap() for n, a in arrays.items()]
    out = nc.dram_tensor("out_rows", (BATCH * SEQ, C), mybir.dt.float32, kind="ExternalOutput").ap()
    sandwich_kernel(nc, *args, out)
    r = run_bass_kernel_spmd(nc, [{f"{n}_in": a for n, a in arrays.items()}], core_ids=[0])
    return r.results[0]["out_rows"].reshape(BATCH, SEQ, C)
```

```python
import concourse.bass as bass
from concourse import mybir
from contextlib import ExitStack

BATCH, SEQ, C = 2, 4096, 512
P = 128
KT = C // P
TILES = SEQ // P
GT = 4
GROUPS = TILES // GT
H1, D1 = 16, 32
H2, D2 = 8, 64
PAIRS = H2 // 2
NEXP = 4
REGION = 12804
PATHS = 1 + NEXP
LORA, GLR = 64, 16
ROW_G, ROW_ONE = LORA, LORA + 2 * GLR
HALF = P // 2
NORMALIZER = 16.0
EPS = 1e-5
EPS_Z = 1.1920928955078125e-07
W_SCALE = 64.0
LS_SCALE = 16.0
S_SCALE = 8.0
REGION2 = 13056
ACT_SET_LN_EXP = 6

CONSTS = {}
_at = 0
for _name, _n in (("ident", P), ("causal", P), ("centred", P), ("halves", 2), ("blocks", P), ("sel_den", KT * P),
                  ("sel_bc", KT * P), ("score", NEXP), ("one_rows", 1), ("ones", P),
                  ("take_low", 1), ("take_high", 1)):
    CONSTS[_name] = (_at, _at + _n)
    _at += _n
N_CONSTS = _at
L_COLS = 2 * P + NEXP


def sandwich_kernel(nc, x_d, wqkv_d, wproj_d, bproj_d, wb_d, wl_d, ws_d, wo_d, nw_d, consts_d, out_d):
    f32, f16 = mybir.dt.float32, mybir.dt.float16
    ALU = mybir.AluOpType
    ACT = mybir.ActivationFunctionType
    X = mybir.AxisListType.X
    q_d = nc.dram_tensor("q_cols", [BATCH * TILES, P, KT * P], f32, kind="Internal").ap()
    x_g = x_d.rearrange("(g t p) c -> g p t c", p=P, t=GT)
    x_p = x_d.rearrange("(j a p) c -> j a p c", p=P, a=2)
    out_p = out_d.rearrange("(j a p) c -> j a p c", p=P, a=2)
    q_p = q_d.rearrange("(j a) p c -> j a p c", a=2)
    q_g = q_d.rearrange("(g t) p c -> g t p c", t=GT)

    with ExitStack() as ctx:
        def sb(name, *shape, dt=f32):
            return ctx.enter_context(nc.sbuf_tensor(name, [P, *shape], dt))

        wqkv = sb("wqkv", 2, KT, 3 * C, dt=f16)
        bproj = sb("bproj", C)
        wb = sb("wb", 2, KT, 3 * C, dt=f16)
        wl = sb("wl", 2, KT, L_COLS, dt=f16)
        ws = sb("ws", 2, 5, C, dt=f16)
        wo = sb("wo", 2, KT, C, dt=f16)
        nw = sb("nw", 1)
        cst = sb("cst", N_CONSTS)
        zero_eps = sb("zero_eps", 1)
        eps_scaled = sb("eps_scaled", 1)
        ident16 = sb("ident16", P, dt=f16)

        def const(name):
            a, b = CONSTS[name]
            return cst[:, a:b]

        ident, causal, centred, halves = const("ident"), const("causal"), const("centred"), const("halves")
        blocks, score, one_rows, ones = const("blocks"), const("score"), const("one_rows"), const("ones")
        sel_den = const("sel_den").rearrange("p (g m) -> p g m", g=KT)
        sel_bc = const("sel_bc").rearrange("p (g m) -> p g m", g=KT)
        CTXW = P + 1
        mix = sb("mix", KT, C)
        kden = sb("kden", KT, P)

        region = sb("region", REGION)
        region2 = sb("region2", REGION2)
        cursor = [0, 0]

        def cut(*shape, own=0, dt=f32):
            n = 1
            for k in shape:
                n *= k
            words = n // 2 if dt == f16 else n
            a = (region, region2)[own][:, cursor[own]:cursor[own] + words]
            cursor[own] += words
            if dt == f16:
                a = a.bitcast(f16)
            if len(shape) == 1:
                return a
            names = "abcd"[:len(shape)]
            return a.rearrange(f"p ({' '.join(names)}) -> p {' '.join(names)}", **dict(zip(names, shape)))

        xn4 = cut(2, GT, C, dt=f16)
        xT4 = cut(2, 2, KT, GT * P, dt=f16)
        q4 = cut(GT, KT, P)
        kk, vv = cut(C), cut(KT, CTXW)
        xf4 = cut(GT, C)
        ctx_sum, ctx_blk = cut(KT, CTXW), cut(KT, P)
        assert cursor[0] <= REGION, cursor
        cursor[0] = GT * C
        w_in = cut(KT, 3 * C)
        cursor[0] = 0
        y, xn = cut(C), cut(2, C, dt=f16)
        xc = y
        xnT, qz = cut(2, KT, P, dt=f16), cut(KT, P)
        logit_s, lowf = cut(4), cut(2, P)
        low = cut(4, P, dt=f16)
        gch = cut(3 * C)
        logsig = cut(3, C)
        ls16 = gch[:, 0:2 * C].bitcast(f16).rearrange("p (x a b) -> p x a b", x=2, a=2)
        v, vm = cut(C), cut(NEXP, C)
        ep1, em1, ep2, em2 = cut(C), cut(C), cut(C), cut(C)
        q1g, k1g, q2g, k2g = ep1, em1, ep2, em2
        kd = cut(C)
        q1T, k1T, q2T, k2T = cut(PAIRS, P), cut(PAIRS, P), cut(PAIRS, P), cut(PAIRS, P)
        assert cursor[0] <= REGION, cursor
        qm = cut(NEXP, PAIRS, P, own=1)
        am1, am2 = cut(2, PAIRS, P, own=1), cut(2, PAIRS, P, own=1)
        state = cut(PAIRS, PATHS, P, own=1)
        carry = cut(PAIRS, PATHS, D2, own=1)
        sil, x1 = cut(2, C, own=1), cut(2, C, own=1)
        loaded_at = cursor[1]
        xb, qb, ob = cut(2, C, own=1), cut(2, KT, P, own=1), cut(2, C, own=1)
        assert cursor[1] <= REGION2, cursor
        cursor[1] = loaded_at
        x4 = cut(GT, C, own=1)
        cursor[1] = 0
        wb_in, wl_in, ws_in = cut(KT * 3 * C, own=1), cut(KT * L_COLS, own=1), cut(5 * C, own=1)
        assert cursor[1] <= loaded_at, cursor
        wo_in = mix.rearrange("p a b -> p (a b)")
        cursor[1] = 0
        wproj = cut(KT, C, own=1)
        decay = sb("decay", PAIRS, PATHS)
        exs = sb("exs", 2, PAIRS, PATHS, 2)
        og, og16, ogT = sb("og", C), sb("og16", 2, C, dt=f16), sb("ogT", 2, KT, P, dt=f16)
        osq = og
        same_c, same_d = sb("same_c", P), sb("same_d", P, dt=f16)
        centred16, halves16 = sb("centred16", P, dt=f16), sb("halves16", 2, dt=f16)
        mb = sb("mb", NEXP, P)
        lab_i = sb("lab_i", P)
        z = sb("z", P)
        st = sb("st", 3, 6)
        mv = sb("mv", 3, 2)
        lnv = sb("lnv", 3, 1)
        rstd = sb("rstd", 3, 1)
        lnv1, rstd1 = sb("lnv1", GT, 1), sb("rstd1", GT, 1)
        st1, mv1 = sb("st1", GT, 6), sb("mv1", GT, 2)
        lmax, ldiff, lexp, lsum, rr, rq = sb("lmax", 1), sb("ldiff", 4), sb("lexp", 4), sb("lsum", 1), sb("rr", 1), sb("rq", 1)
        lscore, lab, m4, hm = sb("lscore", 4), sb("lab", 1), sb("m4", 4), sb("hm", NEXP, 2, dt=f16)
        kmax, ksum, krec, kfac = sb("kmax", H2), sb("ksum", H2), sb("krec", H2), sb("kfac", H2)
        oms, oln, ors = sb("oms", H2), sb("oln", H2), sb("ors", H2)

        psum = ctx.enter_context(nc.psum_tensor("psum", [P, 8, 512], f32))
        bank = [psum[:, i, :] for i in range(8)]
        bank16 = [x.bitcast(f16) for x in bank]

        sems = {}

        def S(name):
            if name not in sems:
                sems[name] = ctx.enter_context(nc.semaphore(name))
            return sems[name]

        CREDITS = {
            "scalar": ["xT4_full", "kv0_full", "kv1_full", "q_read",
                       "rstd1_ok", "xnT_ok", "low1_ok", "low0_ok", "lexp_ok", "abs_ok", "ex_ok", "ln_ok", "sig_ok",
                       "v_ok", "ke_ok", "e1_ok", "e2_ok", "exs_ok", "q1T_ok", "k1T_ok", "q2T_ok", "k2T_ok",
                       "osq_ok", "ogT_ok"],
            "vector": ["xn4_ok", "xf4_ok", "low_ok", "ctx_ok", "y_ok", "x1_ok", "xn_ok", "am1_ok", "am2_ok", "carry_ok", "labi_ok",
                       "same_ok", "mb_ok", "ls_ok", "lsl_ok", "sil_ok", "kd_ok", "kr_ok", "k1g_ok", "q1g_ok", "q2g_ok", "k2g_ok",
                       "z_ok", "qz_ok", "on_ok", "og_ok", "obn_ok", "out_ok", "hm_ok"],
            "tensor": ["xT4_pe", "q_pe", "kv_done", "ctx_tile_pe", "y_pe", "tr_pe", "a_pe", "t_pe", "u_pe", "low_pe",
                       "inter_pe", "rx_pe", "g_pe", "o_pe", "q2_pe", "k1_pe", "k2_pe", "q1_pe", "cum1_pe", "cum_pe", "sum_pe",
                       "den_pe", "og_pe", "bc_pe", "wo_pe", "v_pe"],
            "gpsimd": ["qm_ok", "am_ok", "vm_ok", "state_ok"],
        }
        for names in CREDITS.values():
            for name in names:
                S(name)

        def cur(n):
            return n + 2

        def prev(n):
            return n + 1

        def loads(n, p):
            return (n - p) * 8 + 16

        def wait_alone(eng, sem, value):
            eng.wait_ge(sem, value)
            eng.nop(nofuse=True)

        def whole(ap):
            return ap.rearrange("p a b -> p (a b)")

        def batches(eng):
            return eng.Fori(0, BATCH)

        block = ctx.enter_context(nc.Block())

        @block.sync
        def _(sp):
            def load_group(g):
                sp.dma_start(x4, x_g[bass.ds(g, 1), :, :, :].rearrange("a p t c -> (a p) t c")).then_inc(S("x4_in"), 16)

            def store_q(g):
                wait_alone(sp, S("q_read"), g * KT + KT + 1)
                for t in range(GT):
                    sp.dma_start(q_g[bass.ds(g, 1), t, :, :].rearrange("a p c -> (a p) c"),
                                 q4[:, t, :, :].rearrange("p a b -> p (a b)")).then_inc(S("q4_out"), 16)

            def load(j, p):
                sp.dma_start(xb[:, p, :], x_p[bass.ds(j, 1), p, :, :].rearrange("a p c -> (a p) c")).then_inc(S(f"xb{p}_in"), 16)
                sp.dma_start(qb[:, p, :, :].rearrange("p a b -> p (a b)"),
                             q_p[bass.ds(j, 1), p, :, :].rearrange("a p c -> (a p) c")).then_inc(S(f"qb{p}_in"), 16)

            def store(j, p):
                wait_alone(sp, S("out_ok"), cur(j * 2 + p))
                sp.dma_start(out_p[bass.ds(j, 1), p, :, :].rearrange("a p c -> (a p) c"), ob[:, p, :]).then_inc(S(f"out{p}"), 16)

            sp.dma_start(cst[:, :], consts_d).then_inc(S("consts_in"), 16)
            for k in range(KT):
                sp.dma_start(w_in[:, k, :], wqkv_d[:, k, :]).then_inc(S(f"wqkv{k}_in"), 16)
            for name in ("q4_out", "out0", "out1"):
                sp.sem_inc(S(name), 1)
            with batches(sp) as b:
                g0 = b * GROUPS
                wait_alone(sp, S("x1_ok"), b * TILES + 1)
                wait_alone(sp, S("qz_ok"), b * TILES + 1)
                load_group(g0)
                with sp.Fori(b * GROUPS, b * GROUPS + GROUPS - 1) as g:
                    wait_alone(sp, S("xf4_ok"), cur(g))
                    load_group(g + 1)
                    store_q(g)
                wait_alone(sp, S("xf4_ok"), cur(g0 + GROUPS - 1))
                store_q(g0 + GROUPS - 1)
                wait_alone(sp, S("q4_out"), (b + 1) * (16 * GT * GROUPS) + 1)
                j0 = b * (TILES // 2)
                for p in range(2):
                    load(j0, p)
                with sp.Fori(b * (TILES // 2) + 1, b * (TILES // 2) + TILES // 2) as j:
                    for p in range(2):
                        wait_alone(sp, S("x1_ok"), j * 2 + p)
                        wait_alone(sp, S("qz_ok"), j * 2 + p)
                        load(j, p)
                        store(j - 1, p)
            for p in range(2):
                wait_alone(sp, S(f"out{p}"), BATCH * (TILES // 2 * 16) + 1)

        @block.tensor
        def _(pe):
            mm = nc.tensor.matmul
            for name in CREDITS["tensor"]:
                pe.sem_inc(S(name), 1)
            pe.wait_ge(S("setup"), 1)

            def mm3(out, lhs, rhs, start, stop):
                mm(out, lhs(0), rhs(0), start=start, stop=False)
                mm(out, lhs(0), rhs(1), start=False, stop=False)
                return mm(out, lhs(1), rhs(0), start=False, stop=stop)

            def den(n, p, back=False):
                pe.wait_ge(S(f"qb{p}_in"), loads(n, p))
                if back:
                    pe.wait_ge(S("on_ok"), prev(n - 1))
                else:
                    pe.wait_ge(S("out_ok"), n)
                for g in range(KT):
                    last = mm(bank[4][:, 0:P], kden[:, g, :], qb[:, p, g, :], start=(g == 0), stop=(g == KT - 1))
                last.then_inc(S("den_pe"), 1)

            def bc(n, ahead=True):
                pe.wait_ge(S("z_ok"), cur(n))
                if ahead:
                    pe.wait_ge(S("sil_ok"), prev(n))
                for g in range(KT):
                    last = mm(bank[7][:, g * P:(g + 1) * P], sel_bc[:, g, :], z[:, :], start=True, stop=True)
                last.then_inc(S("bc_pe"), 1)

            def y_mm(n):
                pe.wait_ge(S("qz_ok"), cur(n))
                pe.wait_ge(S("e2_ok"), prev(n))
                for g in range(KT):
                    last = mm(bank[6], qz[:, g, :], mix[:, g, :], start=(g == 0), stop=(g == KT - 1))
                last.then_inc(S("y_pe"), 1)

            def xn_transpose(n):
                pe.wait_ge(S("xn_ok"), cur(n))
                for g in range(KT):
                    for part in range(2):
                        at = (part * KT + g) * P
                        last = nc.tensor.transpose(bank16[7][:, at:at + P], xn[:, part, g * P:(g + 1) * P], ident16[:, :])
                last.then_inc(S("t_pe"), 1)

            def low_rank(n):
                pe.wait_ge(S("xnT_ok"), cur(n))
                for part in range(2):
                    for g in range(KT):
                        mm3(bank[7][:, part * P:(part + 1) * P], lambda x: wl[:, x, g, part * P:(part + 1) * P],
                            lambda x: xnT[:, x, g, :], g == 0, g == KT - 1)
                for g in range(KT):
                    last = mm3(bank[7][:, 2 * P:2 * P + NEXP], lambda x: xnT[:, x, g, :], lambda x: wl[:, x, g, 2 * P:],
                               g == 0, g == KT - 1)
                last.then_inc(S("low_pe"), 1)

            def label_bc(n):
                pe.wait_ge(S("labi_ok"), cur(n))
                pe.wait_ge(S("am2_ok"), prev(n))
                mm(bank[0][:, 0:P], ones, lab_i[:, :], start=True, stop=True).then_inc(S("rx_pe"), 1)

            def second(out, which, k):
                if which == 1:
                    return mm(out, low[:, 1, :], ws[:, 0, k, :], start=True, stop=True)
                h = slice(0, LORA) if which < 3 else slice(LORA, P)
                mm(out, low[:, which, :], ws[:, 0, k, :], start=True, stop=False)
                return mm(out, low[h, which, :], ws[h, 1, k, :], start=False, stop=True)

            def gates(n):
                pe.wait_ge(S("low_ok"), cur(n))
                pe.wait_ge(S("low0_ok"), cur(n))
                for k, which in ((0, 1), (1, 1), (2, 0)):
                    last = second(bank[5 + k], which, k)
                last.then_inc(S("g_pe"), 1)

            def wide(n, where, w0, done):
                for g in range(KT):
                    last = mm3(bank[where], lambda x: xnT[:, x, g, :], lambda x: wb[:, x, g, w0:w0 + C], g == 0, g == KT - 1)
                last.then_inc(S(done), 1)

            def project_v(n):
                pe.wait_ge(S("carry_ok"), prev(n))
                wide(n, 1, 2 * C, "v_pe")

            def project_q2(n):
                pe.wait_ge(S("mb_ok"), cur(n))
                second(bank[0], 2, 3).then_inc(S("q2_pe"), 1)

            def project_k(n):
                wide(n, 2, C, "k1_pe")
                pe.wait_ge(S("v_ok"), cur(n))
                second(bank[1], 3, 4).then_inc(S("k2_pe"), 1)

            def cumulate(n):
                pe.wait_ge(S("lsl_ok"), cur(n))
                pe.wait_ge(S("same_ok"), cur(n))
                pe.wait_ge(S("hm_ok"), cur(n))
                for gate, weights, done in ((0, centred16[:, :], "cum1_pe"), (1, same_d[:, :], "cum_pe")):
                    mm(bank[5 + gate], weights, ls16[:, 0, gate, :], start=True, stop=False)
                    mm(bank[5 + gate], weights, ls16[:, 1, gate, :], start=False, stop=True).then_inc(S(done), 1)

            def half_sums(n):
                pe.wait_ge(S("e1_ok"), cur(n))
                for pr in range(PAIRS):
                    f = slice(pr * P, (pr + 1) * P)
                    for x in range(2):
                        mm(bank[5][:, pr * 10:pr * 10 + 2], ls16[:, x, 0, f], halves16[:, :], start=(x == 0), stop=(x == 1))
                    for x in range(2):
                        last = mm(bank[5][:, pr * 10 + 2:pr * 10 + 10], ls16[:, x, 1, f],
                                  hm[:, :, :].rearrange("p e h -> p (e h)"), start=(x == 0), stop=(x == 1))
                last.then_inc(S("sum_pe"), 1)

            def transposes(n, path):
                dense = ((q1g, 3, "q1g_ok"), (k1g, 2, "k1g_ok"))
                experts = ((q2g, 0, "q2g_ok"), (k2g, 1, "k2g_ok"))
                for src, where, ready in (dense, experts)[path]:
                    pe.wait_ge(S(ready), cur(n))
                    for g in range(PAIRS):
                        last = nc.tensor.transpose(bank[where][:, g * P:(g + 1) * P], src[:, g * P:(g + 1) * P], ident)
                    last.then_inc(S("tr_pe"), 1)

            def scores(n, front):
                for kT, qT, where in ((k1T, q1T, (4, 5)), (k2T, q2T, (6, 0))):
                    if where[0] == 4:
                        pe.wait_ge(S("exs_ok"), cur(n))
                        pe.wait_ge(S("q1T_ok"), cur(n))
                        pe.wait_ge(S("k1T_ok"), cur(n))
                        pe.wait_ge(S("obn_ok"), prev(n))
                    else:
                        if front:
                            pe.wait_ge(S("y_ok"), cur(n + 1))
                        pe.wait_ge(S("q2T_ok"), cur(n))
                        pe.wait_ge(S("k2T_ok"), cur(n))
                    for pr in range(PAIRS):
                        for odd in range(2):
                            h = slice(odd * D2, odd * D2 + D2)
                            last = mm(bank[where[odd]][:, pr * P:(pr + 1) * P], kT[h, pr, :], qT[h, pr, :], start=True, stop=True)
                    last.then_inc(S("a_pe"), 1)

            def state_products(n):
                pe.wait_ge(S("vm_ok"), cur(n))
                for pr in range(PAIRS):
                    mm(bank[1][:, pr * P:(pr + 1) * P], k1g[:, pr * P:(pr + 1) * P], v[:, pr * P:(pr + 1) * P], start=True, stop=True)
                for pr in range(PAIRS):
                    for odd in range(2):
                        h = 2 * pr + odd
                        last = mm(psum[odd * D2:odd * D2 + D2, 2 + pr // 2, (pr % 2) * 256:(pr % 2) * 256 + 256],
                                  k2g[:, h * D2:(h + 1) * D2], vm[:, :, h * D2:(h + 1) * D2], start=True, stop=True)
                last.then_inc(S("u_pe"), 1)

            def inter(n, pairs):
                if 0 in pairs:
                    pe.wait_ge(S("state_ok"), cur(n))
                    pe.wait_ge(S("am1_ok"), cur(n))
                    pe.wait_ge(S("qm_ok"), cur(n))
                for pr in pairs:
                    for path in range(PATHS):
                        q = q1T[:, pr, :] if path == 0 else qm[:, path - 1, pr, :]
                        last = mm(bank[4][:, pr * P:(pr + 1) * P], q, state[:, pr, path, :],
                                  start=(pr == 0 and path == 0), stop=False, skip_group_check=True)
                if PAIRS - 1 in pairs:
                    last.then_inc(S("inter_pe"), 1)

            def intra(n):
                pe.wait_ge(S("am_ok"), cur(n))
                for pr in range(PAIRS):
                    for odd in range(2):
                        h = 2 * pr + odd
                        last = mm(bank[4][:, h * D2:(h + 1) * D2], am1[:, odd, pr, :], v[:, h * D2:(h + 1) * D2],
                                  start=False, stop=True, skip_group_check=True)
                last.then_inc(S("o_pe"), 1)

            def og_transpose(n, ahead):
                pe.wait_ge(S("og_ok"), cur(n))
                if ahead:
                    pe.wait_ge(S("z_ok"), cur(n + 2))
                for g in range(KT):
                    for part in range(2):
                        at = (part * KT + g) * P
                        last = nc.tensor.transpose(bank16[4][:, at:at + P], og16[:, part, g * P:(g + 1) * P], ident16[:, :])
                last.then_inc(S("og_pe"), 1)

            def out_mm(n):
                pe.wait_ge(S("ogT_ok"), cur(n))
                for g in range(KT):
                    last = mm3(bank[4], lambda x: ogT[:, x, g, :], lambda x: wo[:, x, g, :], g == 0, g == KT - 1)
                last.then_inc(S("wo_pe"), 1)

            def step(n, p, front=True, back=True, ahead=True):
                m = n - 1
                if front:
                    y_mm(n)
                if back:
                    transposes(m, 0)
                    transposes(m, 1)
                    scores(m, front)
                    state_products(m)
                if front:
                    xn_transpose(n)
                if back:
                    inter(m, range(PAIRS // 2))
                if front:
                    low_rank(n)
                if back:
                    inter(m, range(PAIRS // 2, PAIRS))
                    intra(m)
                if front:
                    gates(n)
                    label_bc(n)
                    project_v(n)
                    project_q2(n)
                if ahead:
                    den(n + 1, 1 - p, back)
                if front:
                    project_k(n)
                    wide(n, 3, 0, "q1_pe")
                if back:
                    og_transpose(m, ahead)
                if front:
                    cumulate(n)
                if ahead:
                    bc(n + 1)
                if back:
                    out_mm(m)
                if front:
                    half_sums(n)

            with batches(pe) as b:
                def transpose4(g, t):
                    if t == 0:
                        pe.wait_ge(S("xn4_ok"), cur(g))
                    pe.wait_ge(S("xT4_full"), g * GT + max(t, 1))
                    for k in range(KT):
                        for part in range(2):
                            at = (part * KT + k) * P
                            last = nc.tensor.transpose(bank16[t % 2][:, at:at + P], xn4[:, part, t, k * P:(k + 1) * P], ident16[:, :])
                    last.then_inc(S("xT4_pe"), 1)

                def context(g, t):
                    pe.wait_ge(S("kv0_full"), g * GT + t + 2)
                    pe.wait_ge(S("kv1_full"), g * GT + t + 2)
                    if t == 0:
                        pe.wait_ge(S("ctx_ok"), prev(g))
                    for h in range(KT):
                        last = mm(bank[6 + h // 2][:, (h % 2) * CTXW:(h % 2 + 1) * CTXW], kk[:, h * P:(h + 1) * P], vv[:, h, :],
                                  start=(t == 0 and h % 2 == 0), stop=(t == GT - 1), skip_group_check=True)
                    last.then_inc(S("ctx_tile_pe"), 1)

                def group(g, p, ahead=True):
                    pe.wait_ge(S("xT4_full"), g * GT + GT + 1)
                    pe.wait_ge(S("q_read"), g * KT + 1)
                    for m in range(KT):
                        if m >= 2:
                            pe.wait_ge(S("q_read"), g * KT + m)
                        for k in range(KT):
                            last = mm3(bank[2 + m % 2], lambda x: wqkv[:, x, k, m * P:(m + 1) * P], lambda x: xT4[:, p, x, k, :],
                                       k == 0, k == KT - 1)
                        last.then_inc(S("q_pe"), 1)
                    for t in range(GT):
                        for side in range(2):
                            pe.wait_ge(S(f"kv{side}_full"), g * GT + t + 1)
                            for k in range(KT):
                                last = mm3(bank[4 + side], lambda x: xT4[:, p, x, k, t * P:(t + 1) * P],
                                           lambda x: wqkv[:, x, k, C * (1 + side):C * (2 + side)], k == 0, k == KT - 1)
                            last.then_inc(S("kv_done"), 1)
                            if side == 0:
                                if t > 0:
                                    context(g, t - 1)
                                if ahead:
                                    transpose4(g + 1, t)
                    context(g, GT - 1)

                g0 = b * GROUPS
                for t in range(GT):
                    transpose4(g0, t)
                with pe.Fori(b * GROUPS, b * GROUPS + GROUPS - 2, 2) as g:
                    group(g, 0)
                    group(g + 1, 1)
                group(g0 + GROUPS - 2, 0)
                group(g0 + GROUPS - 1, 1, ahead=False)
                pe.wait_ge(S("ctx_blk_ok"), b + 1)
                for g in range(KT):
                    last = nc.tensor.transpose(bank[0][:, g * P:(g + 1) * P], ctx_blk[:, g, :], ident)
                last.then_inc(S("ctx_blk_pe"), 1)
                pe.wait_ge(S("ctxT_ok"), b + 1)
                pe.wait_ge(S("wproj_in"), b * 16 + 16)
                for g in range(KT):
                    mm(bank[1 + g], ctx_sum[:, g, 0:P], wproj[:, g, :], start=True, stop=True).then_inc(S("mix_pe"), 1)
                pe.wait_ge(S("mix_ok"), b + 1)
                n0 = b * TILES
                den(n0, 0)
                bc(n0, ahead=False)
                step(n0, 0, back=False)
                with pe.Fori(b * TILES + 1, b * TILES + TILES - 1, 2) as n:
                    step(n, 1)
                    step(n + 1, 0)
                step(n0 + TILES - 1, 1, ahead=False)
                step(n0 + TILES, 0, front=False, ahead=False)

        @block.scalar
        def _(act):
            ac = nc.scalar.activation
            act.add_instruction(mybir.InstLoadActFuncSet(name=nc.get_next_instruction_name(), act_func_set_id=ACT_SET_LN_EXP,
                                                         ins=[], outs=[]))
            for name in CREDITS["scalar"]:
                act.sem_inc(S(name), 1)
            for k in range(KT):
                act.wait_ge(S(f"wqkv{k}_in"), 16)
                ac(wqkv[:, 0, k, :], w_in[:, k, :], ACT.Copy, scale=W_SCALE).then_inc(S("wqkv_high"), 1)
            act.wait_ge(S("setup"), 1)

            def rstd_of(n, k, done_stat, eps=zero_eps):
                act.wait_ge(S(done_stat), n + 1)
                ac(lnv[:, k, :], mv[:, k, 1:2], ACT.Ln, bias=eps[:, :]).then_inc(S(f"lnv{k}_ok"), 1)
                act.wait_ge(S(f"lnv{k}_ok"), n + 1)
                ac(rstd[:, k, :], lnv[:, k, :], ACT.Exp, scale=-0.5).then_inc(S(f"rstd{k}"), 1)

            def to_cols(n, dst, where, k, done):
                act.wait_ge(S("tr_pe"), n * 4 + 2 + k)
                ac(dst.rearrange("p a b -> p (a b)"), bank[where], ACT.Copy).then_inc(S(done), 1)

            def front_norm1(n):
                rstd_of(n, 0, "mv0_ok")

            def front_norm2(n):
                rstd_of(n, 1, "mv1_ok")

            def front_low(n):
                act.wait_ge(S("t_pe"), cur(n))
                act.wait_ge(S("q1_pe"), prev(n))
                ac(xnT.rearrange("p x a b -> p (x a b)"), bank16[7], ACT.Copy).then_inc(S("xnT_ok"), 1)
                act.wait_ge(S("low_pe"), cur(n))
                act.wait_ge(S("low_ok"), prev(n))
                ac(lowf[:, 0, :], bank[7][:, 0:P], ACT.Identity, bias=one_rows, scale=1.0 / (W_SCALE * S_SCALE))
                ac(lowf[:, 1, :], bank[7][:, P:2 * P], ACT.Copy, scale=1.0 / (W_SCALE * S_SCALE)).then_inc(S("low1_ok"), 1)
                ac(logit_s, bank[7][:, 2 * P:2 * P + NEXP], ACT.Copy, scale=1.0 / W_SCALE).then_inc(S("low0_ok"), 1)
                act.wait_ge(S("ldiff_ok"), n + 1)
                ac(lexp[:, :], ldiff[:, :], ACT.Exp, accum_out=lsum[:, :]).then_inc(S("lexp_ok"), 1)

            def front_gates(n, part):
                if part == 1:
                    act.wait_ge(S("abs_ok"), cur(n))
                    ac(gch, gch, ACT.Exp, scale=-1.0).then_inc(S("ex_ok"), 1)
                    act.wait_ge(S("ex_ok"), cur(n))
                    ac(gch, gch, ACT.Ln, bias=1.0).then_inc(S("ln_ok"), 1)
                    return
                act.wait_ge(S("g_pe"), cur(n))
                act.wait_ge(S("ls_ok"), prev(n))
                ac(gch, psum[:, 5:8, :].rearrange("p a b -> p (a b)"), ACT.Abs).then_inc(S("abs_ok"), 1)

            def front_sig(n):
                act.wait_ge(S("ls_ok"), cur(n))
                ac(ls16[:, 0].rearrange("p a b -> p (a b)"), logsig[:, 0:2, :].rearrange("p a b -> p (a b)"), ACT.Copy,
                   scale=LS_SCALE).then_inc(S("lsh_ok"), 1)
                ac(logsig[:, 2, :], logsig[:, 2, :], ACT.Exp).then_inc(S("sig_ok"), 1)

            def front_v(n):
                act.wait_ge(S("v_pe"), cur(n))
                act.wait_ge(S("vm_ok"), prev(n))
                ac(v, bank[1], ACT.Copy, scale=1.0 / W_SCALE).then_inc(S("v_ok"), 1)

            def front_ke(n):
                act.wait_ge(S("kd_ok"), cur(n))
                ac(kd, kd, ACT.Exp).then_inc(S("ke_ok"), 1)

            def front_exps(n):
                act.wait_ge(S("cum1_pe"), cur(n))
                act.wait_ge(S("tr_pe"), n * 4 + 1)
                act.wait_ge(S("u_pe"), prev(n))
                ac(ep1, bank[5], ACT.Exp, scale=1.0 / LS_SCALE)
                ac(em1, bank[5], ACT.Exp, scale=-1.0 / LS_SCALE).then_inc(S("e1_ok"), 1)
                act.wait_ge(S("cum_pe"), cur(n))
                ac(ep2, bank[6], ACT.Exp, scale=1.0 / LS_SCALE)
                ac(em2, bank[6], ACT.Exp, scale=-1.0 / LS_SCALE).then_inc(S("e2_ok"), 1)

            def front_exs(n, p):
                act.wait_ge(S("sum_pe"), cur(n))
                act.wait_ge(S("state_ok"), prev(n))
                ac(exs[:, p, :, :, :].rearrange("p a b c -> p (a b c)"), bank[5][:, 0:PAIRS * 10], ACT.Exp,
                   scale=1.0 / LS_SCALE).then_inc(S("exs_ok"), 1)

            def back_transposed(n):
                act.wait_ge(S("inter_pe"), prev(n))
                to_cols(n, q1T, 3, 0, "q1T_ok")
                act.wait_ge(S("a_pe"), n * 2 + 1)
                to_cols(n, k1T, 2, 1, "k1T_ok")

            def back_transposed2(n):
                act.wait_ge(S("qm_ok"), prev(n))
                to_cols(n, q2T, 0, 2, "q2T_ok")
                to_cols(n, k2T, 1, 3, "k2T_ok")

            def back_square(n):
                act.wait_ge(S("o_pe"), cur(n))
                act.wait_ge(S("og_ok"), prev(n))
                ac(osq[:, :], bank[4], ACT.Square).then_inc(S("osq_ok"), 1)

            def back_rms(n):
                act.wait_ge(S("oms_ok"), n + 2)
                ac(oln[:, :], oms[:, :], ACT.Ln, bias=zero_eps[:, :], scale=1.0 / D2).then_inc(S("oln_ok"), 1)
                act.wait_ge(S("oln_ok"), n + 1)
                ac(ors[:, :], oln[:, :], ACT.Exp, scale=-0.5).then_inc(S("ors_ok"), 1)

            def back_og(n):
                act.wait_ge(S("og_pe"), cur(n))
                act.wait_ge(S("wo_pe"), prev(n))
                ac(ogT[:, :, :, :].rearrange("p x a b -> p (x a b)"), bank16[4], ACT.Copy).then_inc(S("ogT_ok"), 1)

            def back_norm3(n):
                rstd_of(n, 2, "mv2_ok", eps_scaled)

            def step(n, p, front=True, back=True):
                m = n - 1
                if back:
                    back_transposed(m)
                    back_transposed2(m)
                if front:
                    front_norm1(n)
                    front_norm2(n)
                    front_low(n)
                if back:
                    back_square(m)
                if front:
                    front_gates(n, 0)
                if back:
                    back_rms(m)
                if front:
                    front_gates(n, 1)
                    front_v(n)
                    front_sig(n)
                if back:
                    back_og(m)
                if front:
                    front_ke(n)
                    front_exps(n)
                    front_exs(n, p)
                if back:
                    back_norm3(m)

            with batches(act) as b:
                def norm4(g):
                    act.wait_ge(S("mv1_all"), g + 1)
                    ac(lnv1[:, :, :], mv1[:, :, 1:2], ACT.Ln, bias=zero_eps[:, :]).then_inc(S("lnv_all"), 1)
                    act.wait_ge(S("lnv_all"), g + 1)
                    ac(rstd1[:, :, :], lnv1[:, :, :], ACT.Exp, scale=-0.5).then_inc(S("rstd1_all"), 1)

                def full4(g, p, t):
                    act.wait_ge(S("xT4_pe"), g * GT + t + 2)
                    ac(xT4[:, p, :, :, t * P:(t + 1) * P].rearrange("p x k c -> p (x k) c"),
                       bank16[t % 2].rearrange("p (k c) -> p k c", k=2 * KT), ACT.Copy).then_inc(S("xT4_full"), 1)

                def group(g, p, ahead=True):
                    act.wait_ge(S("q4_out"), g * (16 * GT) + 1)
                    for m in range(KT):
                        act.wait_ge(S("q_pe"), g * KT + m + 2)
                        ac(q4[:, :, m, :], bank[2 + m % 2].rearrange("p (t c) -> p t c", t=GT), ACT.Relu,
                           scale=1.0 / W_SCALE).then_inc(S("q_read"), 1)
                        if ahead and m == 0:
                            norm4(g + 1)
                    for t in range(GT):
                        act.wait_ge(S("kv_done"), 2 * (g * GT + t) + 2)
                        act.wait_ge(S("ctx_tile_pe"), g * GT + t + 1)
                        ac(kk, bank[4], ACT.Relu, scale=1.0 / W_SCALE).then_inc(S("kv0_full"), 1)
                        if ahead:
                            full4(g + 1, 1 - p, t)
                        act.wait_ge(S("kv_done"), 2 * (g * GT + t) + 3)
                        ac(vv[:, :, 0:P], bank[5].rearrange("p (k c) -> p k c", k=KT), ACT.Copy,
                           scale=1.0 / W_SCALE).then_inc(S("kv1_full"), 1)

                g0 = b * GROUPS
                norm4(g0)
                for t in range(GT):
                    full4(g0, 0, t)
                with act.Fori(b * GROUPS, b * GROUPS + GROUPS - 2, 2) as g:
                    group(g, 0)
                    group(g + 1, 1)
                group(g0 + GROUPS - 2, 0)
                group(g0 + GROUPS - 1, 1, ahead=False)
                act.wait_ge(S("ctx_blk_pe"), b + 1)
                ac(ctx_sum[:, :, 0:P], bank[0].rearrange("p (k c) -> p k c", k=KT), ACT.Copy).then_inc(S("ctxT_ok"), 1)
                for g in range(KT):
                    act.wait_ge(S("mix_pe"), b * KT + g + 1)
                    last = ac(mix[:, g, :], bank[1 + g], ACT.Copy)
                last.then_inc(S("mix_ok"), 1)
                n0 = b * TILES
                step(n0, 0, back=False)
                with act.Fori(b * TILES + 1, b * TILES + TILES - 1, 2) as n:
                    step(n, 1)
                    step(n + 1, 0)
                step(n0 + TILES - 1, 1)
                step(n0 + TILES, 0, front=False)
                for p in range(2):
                    wait_alone(act, S("out_ok"), cur(n0 + TILES - 2 + p))
                    act.dma_start(out_p[bass.ds((b + 1) * (TILES // 2) - 1, 1), p, :, :].rearrange("a p c -> (a p) c"),
                                   ob[:, p, :]).then_inc(S(f"out{p}"), 16)

        @block.gpsimd
        def _(pool):
            for name in CREDITS["gpsimd"]:
                pool.sem_inc(S(name), 1)
            pool.wait_ge(S("setup"), 1)
            pool.nop(nofuse=True)
            for dst, src in ((bproj[:, :], bproj_d), (nw[:, :], nw_d), (wb_in, whole(wb_d)),
                             (wl_in, whole(wl_d)), (ws_in, whole(ws_d)), (wo_in, whole(wo_d))):
                pool.dma_start(dst, src).then_inc(S("weights_in"), 16)
            pool.wait_ge(S("weights_in"), 16 * 6)
            late = ((wb_in, wb, W_SCALE, 1.0), (wl_in, wl, W_SCALE, 1.0), (ws_in, ws, S_SCALE, 1.0), (wo_in, wo, W_SCALE, nw[:, :]))
            for src, dst, scale, by in late:
                last = nc.gpsimd.tensor_scalar(src, src, by, scale, ALU.mult, ALU.mult)
            last.then_inc(S("late_scaled"), 1)
            pool.wait_ge(S("late_scaled"), 1)
            for src, dst, scale, by in late:
                last = nc.gpsimd.tensor_scalar(dst[:, 0, :, :].rearrange("p a b -> p (a b)"), src, 1.0, 1.0, ALU.mult, ALU.mult)
            last.then_inc(S("late_high"), 1)
            pool.wait_ge(S("late_high"), 1)
            for src, dst, scale, by in late:
                last = nc.gpsimd.tensor_tensor(dst[:, 1, :, :].rearrange("p a b -> p (a b)"), src,
                                               dst[:, 0, :, :].rearrange("p a b -> p (a b)"), ALU.subtract)
            last.then_inc(S("late_low"), 1)
            pool.wait_ge(S("late_low"), 1)
            gate_rows = ws_in[:, 0:2 * C]
            nc.gpsimd.tensor_scalar(gate_rows, whole(ws[:, 1, 0:2, :]), const("take_low"), 1.0, ALU.mult, ALU.mult)
            nc.gpsimd.tensor_scalar(whole(ws[:, 0, 0:2, :]), whole(ws[:, 0, 0:2, :]), const("take_high"), 1.0,
                                    ALU.mult, ALU.mult).then_inc(S("late_taken"), 1)
            pool.wait_ge(S("late_taken"), 1)
            nc.gpsimd.tensor_tensor(whole(ws[:, 0, 0:2, :]), whole(ws[:, 0, 0:2, :]), gate_rows, ALU.add).then_inc(S("late_split"), 1)

            def back_qm(n):
                pool.wait_ge(S("q2T_ok"), cur(n))
                pool.wait_ge(S("mb_ok"), cur(n))
                pool.wait_ge(S("state_ok"), cur(n))
                pool.wait_ge(S("inter_pe"), prev(n))
                for e in range(NEXP):
                    last = nc.gpsimd.tensor_tensor(qm[:, e, :, :], q2T, mb[:, e, :].unsqueeze(1).to_broadcast([P, PAIRS, P]), ALU.mult)
                last.then_inc(S("qm_ok"), 1)

            def back_am(n):
                pool.wait_ge(S("am2_ok"), cur(n))
                pool.wait_ge(S("am1_ok"), cur(n))
                nc.gpsimd.tensor_tensor(am1[:, :, :, :], am1[:, :, :, :], am2[:, :, :, :], ALU.add).then_inc(S("am_ok"), 1)

            def front_vm(n):
                pool.wait_ge(S("v_ok"), cur(n))
                pool.wait_ge(S("hm_ok"), cur(n))
                wait_alone(pool, S("u_pe"), prev(n))
                for e in range(NEXP):
                    last = nc.gpsimd.tensor_scalar(vm[:, e, :], v, m4[:, e:e + 1], 1.0, ALU.mult, ALU.mult)
                last.then_inc(S("vm_ok"), 1)

            def front_state(n):
                pool.wait_ge(S("decay_ok"), n + 1)
                pool.wait_ge(S("inter_pe"), prev(n))
                pool.wait_ge(S("carry_ok"), prev(n))
                pool.wait_ge(S("vm_ok"), cur(n))
                for odd, done in ((0, "state_half"), (1, "state_ok")):
                    h = slice(odd * D2, odd * D2 + D2)
                    if odd:
                        pool.wait_ge(S("state_half"), n + 1)
                    nc.gpsimd.tensor_tensor(state[h, :, :, h], carry[h, :, :, :],
                                            decay[h, :, :].unsqueeze(3).to_broadcast([D2, PAIRS, PATHS, D2]),
                                            ALU.mult).then_inc(S(done), 1)

            def step(n, p, front=True, back=True):
                if back:
                    back_qm(n - 1)
                    back_am(n - 1)
                if front:
                    front_vm(n)
                    front_state(n)

            pool.wait_ge(S("late_split"), 1)
            with batches(pool) as b:
                wait_alone(pool, S("out_ok"), b * TILES + 1)
                pool.dma_start(wproj, wproj_d).then_inc(S("wproj_in"), 16)
                n0 = b * TILES
                step(n0, 0, back=False)
                with pool.Fori(b * TILES + 1, b * TILES + TILES - 1, 2) as n:
                    step(n, 1)
                    step(n + 1, 0)
                step(n0 + TILES - 1, 1)
                step(n0 + TILES, 0, front=False)

        @block.vector
        def _(dve):
            ve = nc.vector
            for name in CREDITS["vector"] + ["oms_ok"]:
                dve.sem_inc(S(name), 1)
            ve.memset(zero_eps[:, :], EPS)
            ve.memset(eps_scaled[:, :], EPS * W_SCALE * W_SCALE)
            ve.memset(z[:, :], 0.0)
            ve.memset(exs[:, :, :, :, :], 1.0)
            ve.memset(mv[:, :, :], 1.0)
            dve.wait_ge(S("consts_in"), 16)
            ve.tensor_copy(ident16[:, :], ident)
            ve.tensor_copy(centred16[:, :], centred)
            ve.tensor_copy(halves16[:, :], halves)
            for k in range(KT):
                dve.wait_ge(S(f"wqkv{k}_in"), 16)
                dve.wait_ge(S("wqkv_high"), k + 1)
                last = ve.scalar_tensor_tensor(wqkv[:, 1, k, :], w_in[:, k, :], W_SCALE, wqkv[:, 0, k, :], ALU.mult, ALU.subtract)
            last.then_inc(S("setup"), 1)

            def flat(ap):
                return ap.rearrange("p a b -> p (a b)")

            def heads(ap):
                return ap.rearrange("p (h d) -> p h d", h=H2)

            def wide(ap, n):
                return ap.unsqueeze(2).to_broadcast([ap.shape[0], ap.shape[1], n])

            def stats(n, k, src):
                ve.bn_stats(st[:, k, :], src).then_inc(S(f"st{k}_ok"), 1)
                wait_alone(dve, S(f"st{k}_ok"), n + 1)
                ve.bn_aggr(mv[:, k, :], st[:, k, :]).then_inc(S(f"mv{k}_ok"), 1)

            def normed(n, k, dst, src, done, value):
                dve.wait_ge(S(f"rstd{k}"), n + 1)
                ve.tensor_scalar(dst, src, mv[:, k, 0:1], rstd[:, k, :], ALU.subtract, ALU.mult).then_inc(S(done), 1)
                dve.wait_ge(S(done), value)

            def split(n, dst, src, high, done):
                ve.tensor_copy(dst[:, 0], src).then_inc(S(high), 1)
                dve.wait_ge(S(high), n + 1)
                ve.tensor_tensor(dst[:, 1], src, dst[:, 0], ALU.subtract).then_inc(S(done), 1)

            def front_y(n):
                dve.wait_ge(S("y_pe"), cur(n))
                ve.tensor_tensor(y, bank[6], bproj[:, :], ALU.add).then_inc(S("y_ok"), 1)

            def front_y_stats(n):
                dve.wait_ge(S("y_ok"), cur(n))
                stats(n, 0, y)
                dve.wait_ge(S("mv0_ok"), n + 1)
                ve.tensor_scalar(y, y, mv[:, 0, 0:1], None, ALU.subtract).then_inc(S("yc_ok"), 1)

            def front_residual(n, p):
                dve.wait_ge(S("yc_ok"), n + 1)
                dve.wait_ge(S("rstd0"), n + 1)
                dve.wait_ge(S(f"xb{p}_in"), loads(n, p))
                ve.scalar_tensor_tensor(x1[:, p, :], y, rstd[:, 0, :], xb[:, p, :], ALU.mult, ALU.add).then_inc(S("x1_ok"), 1)
                dve.wait_ge(S("x1_ok"), cur(n))
                stats(n, 1, x1[:, p, :])
                dve.wait_ge(S("mv1_ok"), n + 1)
                ve.tensor_scalar(xc, x1[:, p, :], mv[:, 1, 0:1], None, ALU.subtract).then_inc(S("xc_ok"), 1)

            def front_normed(n):
                dve.wait_ge(S("xc_ok"), n + 1)
                dve.wait_ge(S("rstd1"), n + 1)
                dve.wait_ge(S("t_pe"), prev(n))
                ve.tensor_scalar(xn[:, 0], xc, rstd[:, 1, :], None, ALU.mult).then_inc(S("xnh_ok"), 1)
                dve.wait_ge(S("xnh_ok"), n + 1)
                ve.scalar_tensor_tensor(xn[:, 1], xc, rstd[:, 1, :], xn[:, 0], ALU.mult, ALU.subtract).then_inc(S("xn_ok"), 1)

            def back_masks(n):
                dve.wait_ge(S("a_pe"), n * 2 + 2)
                dve.wait_ge(S("o_pe"), prev(n))
                for odd in range(2):
                    last = ve.tensor_tensor(am1[:, odd, :, :], bank[4 + odd].rearrange("p (a b) -> p a b", a=PAIRS),
                                            causal.unsqueeze(1).to_broadcast([P, PAIRS, P]), ALU.mult)
                last.then_inc(S("am1_ok"), 1)

            def back_masks2(n):
                dve.wait_ge(S("a_pe"), n * 2 + 3)
                dve.wait_ge(S("am_ok"), prev(n))
                for odd in range(2):
                    last = ve.tensor_tensor(am2[:, odd, :, :], bank[(6, 0)[odd]].rearrange("p (a b) -> p a b", a=PAIRS),
                                            same_c[:, :].unsqueeze(1).to_broadcast([P, PAIRS, P]), ALU.mult)
                last.then_inc(S("am2_ok"), 1)

            def back_carry(n):
                dve.wait_ge(S("u_pe"), cur(n))
                dve.wait_ge(S("state_ok"), cur(n))
                for odd in range(2):
                    h = slice(odd * D2, odd * D2 + D2)
                    ve.tensor_tensor(carry[h, :, 0, :], bank[1][h, :].rearrange("p (a b) -> p a b", a=PAIRS)[:, :, h],
                                     state[h, :, 0, h], ALU.add)
                    last = ve.tensor_tensor(carry[h, :, 1:PATHS, :], psum[h, 2:4, :].rearrange("p a (r e d) -> p (a r) e d", r=2, e=NEXP),
                                            state[h, :, 1:PATHS, h], ALU.add)
                last.then_inc(S("carry_ok"), 1)

            def front_low(n):
                dve.wait_ge(S("low1_ok"), cur(n))
                dve.wait_ge(S("k2_pe"), prev(n))
                up, down = slice(0, LORA), slice(LORA, P)
                g, g_low, g_copy = slice(ROW_G, ROW_ONE), slice(0, 2 * GLR), slice(2 * GLR, 4 * GLR)
                ve.tensor_copy(low[up, 0:4:2, :], lowf[up, :, :])
                ve.tensor_copy(low[down, 1:4:2, :], lowf[down, :, :])
                ve.tensor_copy(low[g_copy, 1, :], lowf[g, 0, :]).then_inc(S("lowh_ok"), 1)
                dve.wait_ge(S("lowh_ok"), n + 1)
                ve.tensor_tensor(low[g_low, 1, :], lowf[g, 0, :], low[g, 1, :], ALU.subtract)
                ve.tensor_tensor(low[down, 0:4:2, :], lowf[up, :, :], low[up, 0:4:2, :], ALU.subtract)
                ve.tensor_tensor(low[up, 3, :], lowf[down, 1, :], low[down, 3, :], ALU.subtract).then_inc(S("low_ok"), 1)

            def front_router(n):
                dve.wait_ge(S("low0_ok"), cur(n))
                ve.reduce_max(lmax[:, :], logit_s, X).then_inc(S("lmax_ok"), 1)
                dve.wait_ge(S("lmax_ok"), n + 1)
                ve.tensor_scalar(ldiff[:, :], logit_s, lmax[:, :], None, ALU.subtract).then_inc(S("ldiff_ok"), 1)
                dve.wait_ge(S("ldiff_ok"), n + 1)
                ve.scalar_tensor_tensor(lscore[:, :], ldiff[:, :], 0.0, score, ALU.is_equal, ALU.mult).then_inc(S("lscore_ok"), 1)
                dve.wait_ge(S("lscore_ok"), n + 1)
                ve.reduce_max(lab[:, :], lscore[:, :], X).then_inc(S("lab_ok"), 1)
                dve.wait_ge(S("lab_ok"), n + 1)
                dve.wait_ge(S("rx_pe"), prev(n))
                ve.tensor_scalar(lab_i[:, :], ident, lab[:, :], None, ALU.mult).then_inc(S("labi_ok"), 1)
                dve.wait_ge(S("vm_ok"), prev(n))
                ve.tensor_scalar(m4[:, :], score, lab[:, :], None, ALU.is_equal).then_inc(S("m4_ok"), 1)
                dve.wait_ge(S("m4_ok"), n + 1)
                dve.wait_ge(S("sum_pe"), prev(n))
                ve.tensor_tensor(hm[:, :, :], wide(m4[:, :], 2), halves.unsqueeze(1).to_broadcast([P, NEXP, 2]), ALU.mult).then_inc(S("hm_ok"), 1)
                dve.wait_ge(S("lexp_ok"), cur(n))
                ve.reciprocal(rr[:, :], lsum[:, :]).then_inc(S("rr_ok"), 1)
                dve.wait_ge(S("rr_ok"), n + 1)
                ve.tensor_scalar(rq[:, :], rr[:, :], D2 ** -0.5, None, ALU.mult).then_inc(S("rq_ok"), 1)

            def front_masks(n):
                dve.wait_ge(S("rx_pe"), cur(n))
                dve.wait_ge(S("cum_pe"), prev(n))
                row = bank[0][:, 0:P]
                ve.scalar_tensor_tensor(same_d[:, :], row, lab[:, :], centred, ALU.is_equal, ALU.mult)
                ve.scalar_tensor_tensor(same_c[:, :], row, lab[:, :], causal, ALU.is_equal, ALU.mult).then_inc(S("same_ok"), 1)
                dve.wait_ge(S("qm_ok"), prev(n))
                for e in range(NEXP):
                    last = ve.tensor_scalar(mb[:, e, :], row, float(NEXP - e), None, ALU.is_equal)
                last.then_inc(S("mb_ok"), 1)

            def front_logsig(n):
                dve.wait_ge(S("ln_ok"), cur(n))
                dve.wait_ge(S("sum_pe"), prev(n))
                dve.wait_ge(S("sil_ok"), prev(n))
                ve.scalar_tensor_tensor(flat(logsig), psum[:, 5:8, :].rearrange("p a b -> p (a b)"), 0.0, gch,
                                        ALU.min, ALU.subtract).then_inc(S("ls_ok"), 1)

            def front_sil(n, p):
                dve.wait_ge(S("sig_ok"), cur(n))
                ve.tensor_tensor(sil[:, p, :], bank[7], logsig[:, 2, :], ALU.mult).then_inc(S("sil_ok"), 1)

            def front_lslow(n):
                dve.wait_ge(S("lsh_ok"), n + 1)
                ve.scalar_tensor_tensor(flat(ls16[:, 1]), flat(logsig[:, 0:2, :]), LS_SCALE, flat(ls16[:, 0]),
                                        ALU.mult, ALU.subtract).then_inc(S("lsl_ok"), 1)

            def front_softmax(n):
                dve.wait_ge(S("k2_pe"), cur(n))
                ve.reduce_max(kmax[:, :], heads(bank[1]), X).then_inc(S("kmax_ok"), 1)

            def front_diff(n):
                dve.wait_ge(S("kmax_ok"), n + 1)
                dve.wait_ge(S("kr_ok"), prev(n))
                dve.wait_ge(S("k2g_ok"), prev(n))
                ve.tensor_tensor(heads(kd), heads(bank[1]), wide(kmax[:, :], D2), ALU.subtract).then_inc(S("kd_ok"), 1)

            def front_softmax2(n):
                dve.wait_ge(S("ke_ok"), cur(n))
                ve.reduce_sum(ksum[:, :], heads(kd), X).then_inc(S("ksum_ok"), 1)
                dve.wait_ge(S("ksum_ok"), n + 1)
                ve.reciprocal(krec[:, :], ksum[:, :]).then_inc(S("krec_ok"), 1)
                dve.wait_ge(S("krec_ok"), n + 1)
                ve.tensor_scalar(kfac[:, :], krec[:, :], rr[:, :], None, ALU.mult).then_inc(S("kfac_ok"), 1)

            def front_scaled(n):
                dve.wait_ge(S("kfac_ok"), n + 1)
                ve.tensor_tensor(heads(kd), heads(kd), wide(kfac[:, :], D2), ALU.mult).then_inc(S("kr_ok"), 1)

            def front_gated_1(n):
                dve.wait_ge(S("e1_ok"), cur(n))
                dve.wait_ge(S("q1_pe"), cur(n))
                ve.scalar_tensor_tensor(q1g, bank[3], D2 ** -0.5 / W_SCALE, ep1, ALU.mult, ALU.mult).then_inc(S("q1g_ok"), 1)
                ve.scalar_tensor_tensor(k1g, bank[2], 1.0 / W_SCALE, em1, ALU.mult, ALU.mult).then_inc(S("k1g_ok"), 1)

            def front_gated_q2(n):
                dve.wait_ge(S("e2_ok"), cur(n))
                dve.wait_ge(S("rq_ok"), n + 1)
                ve.scalar_tensor_tensor(q2g, bank[0], rq[:, :], ep2, ALU.mult, ALU.mult).then_inc(S("q2g_ok"), 1)

            def front_gated_k(n):
                dve.wait_ge(S("kr_ok"), cur(n))
                ve.tensor_tensor(k2g, kd, em2, ALU.mult).then_inc(S("k2g_ok"), 1)

            def front_decay(n, p):
                dve.wait_ge(S("exs_ok"), cur(n))
                dve.wait_ge(S("state_ok"), prev(n))
                ve.tensor_tensor(decay[:, :, :], exs[:, 1 - p, :, :, 1], exs[:, p, :, :, 0], ALU.mult).then_inc(S("decay_ok"), 1)

            def ahead_z(n):
                dve.wait_ge(S("den_pe"), cur(n))
                dve.wait_ge(S("bc_pe"), prev(n))
                ve.tensor_scalar(z[0:H1, :], bank[4][0:H1, 0:P], EPS_Z, None, ALU.add).then_inc(S("zd_ok"), 1)
                dve.wait_ge(S("zd_ok"), n + 1)
                ve.reciprocal(z[0:H1, :], z[0:H1, :]).then_inc(S("z_ok"), 1)

            def ahead_qz(n, p):
                dve.wait_ge(S("bc_pe"), cur(n))
                dve.wait_ge(S("y_pe"), prev(n))
                ve.tensor_tensor(flat(qz), bank[7], flat(qb[:, p, :, :]), ALU.mult).then_inc(S("qz_ok"), 1)

            def back_norm(n):
                dve.wait_ge(S("osq_ok"), cur(n))
                ve.reduce_sum(oms[:, :], heads(osq[:, :]), X).then_inc(S("oms_ok"), 1)

            def back_normed(n, p):
                dve.wait_ge(S("ors_ok"), n + 1)
                ve.tensor_tensor(heads(og[:, :]), heads(bank[4]), wide(ors[:, :], D2), ALU.mult).then_inc(S("on_ok"), 1)

            def back_gated(n, p):
                dve.wait_ge(S("on_ok"), cur(n))
                ve.tensor_tensor(og[:, :], og[:, :], sil[:, p, :], ALU.mult).then_inc(S("ogf_ok"), 1)

            def back_split(n):
                dve.wait_ge(S("ogf_ok"), n + 1)
                dve.wait_ge(S("og_pe"), prev(n))
                split(n, og16[:, :, :], og[:, :], "ogh_ok", "og_ok")

            def back_stats(n):
                dve.wait_ge(S("wo_pe"), cur(n))
                stats(n, 2, bank[4])

            def back_out(n, p):
                dve.wait_ge(S(f"out{p}"), (n - p) * 8 + 1)
                normed(n, 2, ob[:, p, :], bank[4], "obn_ok", n + 2)
                ve.tensor_tensor(ob[:, p, :], ob[:, p, :], x1[:, p, :], ALU.add).then_inc(S("out_ok"), 1)

            def step(n, p, front=True, back=True, ahead=True):
                m, mp = n - 1, 1 - p
                if front:
                    front_y(n)
                    front_y_stats(n)
                if front:
                    front_residual(n, p)
                    front_normed(n)
                if back:
                    back_masks(m)
                    back_masks2(m)
                    back_carry(m)
                if front:
                    front_low(n)
                    front_router(n)
                if back:
                    back_norm(m)
                if front:
                    front_masks(n)
                if back:
                    back_normed(m, mp)
                    back_gated(m, mp)
                    back_split(m)
                if front:
                    front_logsig(n)
                if ahead:
                    ahead_z(n + 1)
                if front:
                    front_lslow(n)
                    front_softmax(n)
                    front_sil(n, p)
                    front_diff(n)
                    front_softmax2(n)
                    front_gated_1(n)
                if ahead:
                    ahead_qz(n + 1, mp)
                if front:
                    front_gated_q2(n)
                if back:
                    back_stats(m)
                if front:
                    front_decay(n, p)
                    front_scaled(n)
                    front_gated_k(n)
                if back:
                    back_out(m, mp)

            with batches(dve) as b:
                dve.wait_ge(S("out_ok"), b * TILES + 1)
                ve.memset(vv[:, :, P:CTXW], 1.0)
                ve.memset(ctx_sum[:, :, :], 0.0).then_inc(S("ctx_zero"), 1)
                dve.wait_ge(S("ctx_zero"), b + 1)
                def norm4(g):
                    dve.wait_ge(S("x4_in"), g * 16 + 16)
                    for t in range(GT):
                        last = ve.bn_stats(st1[:, t, :], x4[:, t, :])
                    last.then_inc(S("st1_all"), 1)
                    wait_alone(dve, S("st1_all"), g + 1)
                    for t in range(GT):
                        last = ve.bn_aggr(mv1[:, t, :], st1[:, t, :])
                    last.then_inc(S("mv1_all"), 1)
                    dve.wait_ge(S("rstd1_all"), g + 1)
                    for t in range(GT):
                        last = ve.tensor_scalar(xf4[:, t, :], x4[:, t, :], mv1[:, t, 0:1], rstd1[:, t, :], ALU.subtract, ALU.mult)
                    last.then_inc(S("xf4_ok"), 1)
                    dve.wait_ge(S("xf4_ok"), cur(g))
                    dve.wait_ge(S("xT4_pe"), g * GT + 1)
                    ve.tensor_copy(flat(xn4[:, 0]), flat(xf4)).then_inc(S("xh4_ok"), 1)
                    dve.wait_ge(S("xh4_ok"), g + 1)
                    ve.tensor_tensor(flat(xn4[:, 1]), flat(xf4), flat(xn4[:, 0]), ALU.subtract).then_inc(S("xn4_ok"), 1)

                def add_context(g):
                    dve.wait_ge(S("ctx_tile_pe"), g * GT + GT + 1)
                    for k in range(2):
                        last = ve.tensor_tensor(ctx_sum[:, 2 * k:2 * k + 2, :],
                                                bank[6 + k][:, 0:2 * CTXW].rearrange("p (a b) -> p a b", a=2),
                                                ctx_sum[:, 2 * k:2 * k + 2, :], ALU.add)
                    last.then_inc(S("ctx_ok"), 1)

                g0 = b * GROUPS
                norm4(g0)
                with dve.Fori(b * GROUPS, b * GROUPS + GROUPS - 1) as g:
                    norm4(g + 1)
                    add_context(g)
                    dve.wait_ge(S("ctx_ok"), cur(g))
                add_context(g0 + GROUPS - 1)
                dve.wait_ge(S("ctx_ok"), cur(g0 + GROUPS - 1))
                ve.tensor_tensor(kden[:, :, :], sel_den, ctx_sum[:, :, P:CTXW].to_broadcast([P, KT, P]), ALU.mult)
                ve.tensor_tensor(ctx_blk[:, :, :], ctx_sum[:, :, 0:P], blocks.unsqueeze(1).to_broadcast([P, KT, P]), ALU.mult)\
                    .then_inc(S("ctx_blk_ok"), 1)
                dve.wait_ge(S("late_split"), 1)
                ve.memset(state, 0.0)
                ve.memset(carry, 0.0).then_inc(S("carry_zero"), 1)
                dve.wait_ge(S("carry_zero"), b + 1)
                dve.wait_ge(S("ctxT_ok"), b + 1)
                n0 = b * TILES
                ahead_z(n0)
                ahead_qz(n0, 0)
                step(n0, 0, back=False)
                with dve.Fori(b * TILES + 1, b * TILES + TILES - 1, 2) as n:
                    step(n, 1)
                    step(n + 1, 0)
                step(n0 + TILES - 1, 1, ahead=False)
                step(n0 + TILES, 0, front=False, ahead=False)


def layouts(i):
    import numpy as np

    def tiles(w):
        return np.ascontiguousarray(w.reshape(w.shape[0] // P, P, w.shape[1]).transpose(1, 0, 2))

    a = {k: np.asarray(v) for k, v in i.items()}
    low = np.zeros((C, L_COLS), np.float32)
    low[:, 0:LORA] = a["L0_ffn_Wga"]
    low[:, ROW_G:ROW_G + GLR] = a["L0_ffn_Wg1a"]
    low[:, ROW_G + GLR:ROW_ONE] = a["L0_ffn_Wg2a"]
    low[:, P:P + LORA] = a["L0_ffn_Wqa"]
    low[:, P + LORA:2 * P] = a["L0_ffn_Wka"]
    low[:, 2 * P:] = a["L0_ffn_We"]
    second = np.zeros((P, 5, C), np.float32)
    for gate, (w, bias) in enumerate((("L0_ffn_Wg1b", "L0_ffn_bg1"), ("L0_ffn_Wg2b", "L0_ffn_bg2"))):
        for rows in range(0, ROW_ONE, 2 * GLR):
            second[rows + gate * GLR:rows + gate * GLR + GLR, gate] = a[w]
        second[ROW_ONE:ROW_ONE + 2, gate] = a[bias]
    for k, w in ((2, "L0_ffn_Wgb"), (3, "L0_ffn_Wqb"), (4, "L0_ffn_Wkb")):
        second[0:LORA, k] = second[LORA:, k] = a[w]
    cst = np.zeros((P, N_CONSTS), np.float32)
    s, t = np.arange(P)[:, None], np.arange(P)[None, :]

    def put(name, value):
        lo, hi = CONSTS[name]
        cst[:value.shape[0], lo:hi] = value

    put("ident", np.eye(P))
    put("causal", t >= s)
    put("centred", (1.0 * (t >= s) - 1.0 * (s < HALF)) / NORMALIZER)
    put("halves", np.concatenate([s < HALF, s >= HALF], 1) / NORMALIZER)
    put("blocks", s // D1 == t // D1)
    head = np.arange(KT)[:, None] * (P // D1) + np.arange(P)[None, :] // D1
    sel = np.arange(P)[:, None, None] == head[None]
    put("sel_bc", sel.reshape(P, KT * P))
    put("sel_den", sel.transpose(2, 1, 0).reshape(P, KT * P))
    put("score", np.broadcast_to(np.arange(NEXP, 0, -1)[None], (P, NEXP)))
    put("one_rows", (s >= ROW_ONE) / S_SCALE)
    takes_low = ((s >= 2 * GLR) & (s < 4 * GLR)) | (s == ROW_ONE + 1)
    put("take_low", takes_low)
    put("take_high", ~takes_low)
    put("ones", np.ones((P, P)))
    return {
        "x": np.ascontiguousarray(a["L0_attn_x"].reshape(BATCH * SEQ, C)),
        "wqkv": tiles(a["L0_attn_w_qkv"].T),
        "wproj": tiles(a["L0_attn_w_proj"].T),
        "bproj": np.ascontiguousarray(np.broadcast_to(a["L0_attn_b_proj"][None], (P, C))),
        "wb": tiles(np.concatenate([a["L0_ffn_Wq"], a["L0_ffn_Wk"], a["L0_ffn_Wv"]], 1)),
        "wl": tiles(low),
        "ws": second,
        "wo": tiles(a["L0_ffn_Wo"]),
        "nw": np.ascontiguousarray(np.tile(a["L0_ffn_norm_w"], 2)[:, None]),
        "consts": cst,
    }


def kernel(**inputs):
    import numpy as np
    import concourse.bacc as bacc
    from concourse.bass_utils import run_bass_kernel_spmd

    nc = bacc.Bacc("TRN2", target_bir_lowering=False, num_devices=1)
    arrays = layouts(inputs)
    args = [nc.dram_tensor(f"{n}_in", a.shape, mybir.dt.from_np(a.dtype), kind="ExternalInput").ap() for n, a in arrays.items()]
    out = nc.dram_tensor("out_rows", (BATCH * SEQ, C), mybir.dt.float32, kind="ExternalOutput").ap()
    sandwich_kernel(nc, *args, out)
    r = run_bass_kernel_spmd(nc, [{f"{n}_in": a for n, a in arrays.items()}], core_ids=[0])
    return r.results[0]["out_rows"].reshape(BATCH, SEQ, C)
```
